# Optimizing a Trainium2 kernel written in Bass

```python
import numpy as np
import jax
import jax.numpy as jnp

def _softmax(x, axis=-1):
    return jax.nn.softmax(x, axis=axis)

def _gelu(x):
    return jax.nn.gelu(x, approximate=True)

def _silu(x):
    return jax.nn.silu(x)

def _sigmoid(x):
    return jax.nn.sigmoid(x)

def _layernorm(x, axis=-1, eps=1e-05):
    m = jnp.mean(x, axis=axis, keepdims=True)
    v = jnp.var(x, axis=axis, keepdims=True)
    return (x - m) / jnp.sqrt(v + eps)

def _scatter_add(tgt, idx, src, axis=0):
    return tgt.at[idx].add(src)

def _segment_sum(src, seg, n):
    return jax.ops.segment_sum(src, seg, n)
kernel_name = 'mk_flamingo_gated_d1_seqx_r8_cc984e'

def setup_inputs(seed: int=0):
    np.random.seed(seed)
    _w = jnp.asarray

    def _rec_inputs():
        import jax
        import jax.numpy as jnp
        _rk = jax.random.key(seed)
        x = -0.0002928 + 1 * jax.random.normal(jax.random.fold_in(_rk, 1), (8, 256, 128), jnp.float32)
        _lenS = 256 - jax.random.randint(jax.random.fold_in(_rk, 7), (8,), 0, max(1, 256 // 4) + 1, jnp.int32)
        _lenS2 = 256 - jax.random.randint(jax.random.fold_in(_rk, 8), (8,), 0, max(1, 256 // 4) + 1, jnp.int32)
        _ctx_1024P = jax.random.normal(jax.random.fold_in(_rk, 11), (8, 16, 128), jnp.float32)
        _ctx_1024c = jax.random.dirichlet(jax.random.fold_in(_rk, 511), 0.3 * jnp.ones((16,), jnp.float32), (8, 256))
        _ctx_1024t = jnp.einsum('bsk,bkd->bsd', _ctx_1024c, _ctx_1024P)
        _ctx_1024t = _ctx_1024t * jax.lax.rsqrt(jnp.mean(jnp.square(_ctx_1024t)) + 1e-12) * 0.953939
        ctx_1024 = -1.39393e-06 + 0.999914 * (_ctx_1024t + 0.3 * jax.random.normal(jax.random.fold_in(_rk, 611), (8, 256, 128), jnp.float32))
        _g = jax.random.normal(jax.random.fold_in(_rk, 9001), (2, 1), jnp.float32)
        _g = jnp.sign(_g) * jnp.maximum(jnp.abs(_g), 1.0) + (_g == 0) * 1.0
        g_xattn = _g[0]
        g_ffn = _g[1]
        return (x, ctx_1024, g_xattn, g_ffn)
    x, ctx_1024, g_xattn, g_ffn = _rec_inputs()

    def _L0_xattn_setup():
        import jax, jax.numpy as jnp
        import numpy as np
        D_MODEL = 128
        NUM_HEADS = 16
        HEAD_DIM = D_MODEL // NUM_HEADS
        key = jax.random.key(seed)
        ks = jax.random.split(key, 11)
        B, S, D = (2, 256, D_MODEL)
        s = 1.0 / np.sqrt(D)
        inp = {'query': jax.random.normal(ks[0], (B, S, D), jnp.float32), 'key': jax.random.normal(ks[1], (B, S, D), jnp.float32), 'value': jax.random.normal(ks[2], (B, S, D), jnp.float32), 'Wq': jax.random.normal(ks[3], (D, D), jnp.float32) * s, 'bq': jnp.zeros((D,), jnp.float32), 'Wk': jax.random.normal(ks[4], (D, D), jnp.float32) * s, 'bk': jnp.zeros((D,), jnp.float32), 'Wv': jax.random.normal(ks[5], (D, D), jnp.float32) * s, 'bv': jnp.zeros((D,), jnp.float32), 'Wo': jax.random.normal(ks[6], (D, D), jnp.float32) * s, 'bo': jnp.zeros((D,), jnp.float32)}
        return inp
    _L0_xattn_all = _L0_xattn_setup()
    _L0_xattn_in = {k: v for k, v in _L0_xattn_all.items() if k in ('Wq', 'bq', 'Wk', 'bk', 'Wv', 'bv', 'Wo', 'bo')}
    del _L0_xattn_all

    def _L0_ffn_setup():
        import jax, jax.numpy as jnp
        import numpy as np
        H = 128
        E = 8
        B, S = (4, 256)
        key = jax.random.key(seed)
        k1, k2, k3, k4 = jax.random.split(key, 4)
        x = jax.random.normal(k1, (B, S, H), dtype=jnp.float32)
        wg = jax.random.normal(k2, (H, E), dtype=jnp.float32) * 0.02
        W = jax.random.normal(k3, (E, H, H), dtype=jnp.float32) * 0.02
        b = jax.random.normal(k4, (E, H), dtype=jnp.float32) * 0.02
        return {'x': x, 'wg': wg, 'W': W, 'b': b}
    _L0_ffn_all = _L0_ffn_setup()
    _L0_ffn_in = {k: v for k, v in _L0_ffn_all.items() if k in ('wg', 'W', 'b')}
    del _L0_ffn_all
    return {'x': x, 'ctx_1024': ctx_1024, 'g_xattn': g_xattn, 'g_ffn': g_ffn, 'L0_xattn_Wq': _L0_xattn_in['Wq'], 'L0_xattn_bq': _L0_xattn_in['bq'], 'L0_xattn_Wk': _L0_xattn_in['Wk'], 'L0_xattn_bk': _L0_xattn_in['bk'], 'L0_xattn_Wv': _L0_xattn_in['Wv'], 'L0_xattn_bv': _L0_xattn_in['bv'], 'L0_xattn_Wo': _L0_xattn_in['Wo'], 'L0_xattn_bo': _L0_xattn_in['bo'], 'L0_ffn_wg': _L0_ffn_in['wg'], 'L0_ffn_W': _L0_ffn_in['W'], 'L0_ffn_b': _L0_ffn_in['b']}

def reference(x, ctx_1024, g_xattn, g_ffn, L0_xattn_Wq, L0_xattn_bq, L0_xattn_Wk, L0_xattn_bk, L0_xattn_Wv, L0_xattn_bv, L0_xattn_Wo, L0_xattn_bo, L0_ffn_wg, L0_ffn_W, L0_ffn_b):
    import jax
    import jax.numpy as jnp

    def _L0_xattn_ref(query, key, value, Wq, bq, Wk, bk, Wv, bv, Wo, bo):
        import jax, jax.numpy as jnp
        import numpy as np
        D_MODEL = 128
        NUM_HEADS = 16
        HEAD_DIM = D_MODEL // NUM_HEADS
        B, S, D = query.shape
        H, Hd = (NUM_HEADS, HEAD_DIM)
        Q = (query @ Wq.T + bq).reshape(B, S, H, Hd).transpose(0, 2, 1, 3)
        K = (key @ Wk.T + bk).reshape(B, S, H, Hd).transpose(0, 2, 1, 3)
        V = (value @ Wv.T + bv).reshape(B, S, H, Hd).transpose(0, 2, 1, 3)
        scale = 1.0 / jnp.sqrt(jnp.asarray(Hd, Q.dtype))
        scores = jnp.einsum('bhqd,bhkd->bhqk', Q, K) * scale
        attn = jax.nn.softmax(scores, axis=-1)
        out = jnp.einsum('bhqk,bhkd->bhqd', attn, V)
        out = out.transpose(0, 2, 1, 3).reshape(B, S, D)
        return out @ Wo.T + bo

    def _L0_ffn_ref(x, wg, W, b):
        import jax, jax.numpy as jnp
        import numpy as np
        H = 128
        E = 8
        B, S = (4, 256)
        Bb, Ss, Hh = x.shape
        Ee = wg.shape[1]
        T = Bb * Ss
        C = T // Ee
        xt = x.reshape(T, Hh)
        logits = xt @ wg
        probs = jax.nn.softmax(logits, axis=-1)
        idx = jnp.argmax(probs, axis=-1)
        mask = jax.nn.one_hot(idx, Ee, dtype=xt.dtype)
        locations = jnp.cumsum(mask, axis=0) - mask
        mask = mask * (locations < C).astype(xt.dtype)
        gate = jnp.sum(probs * mask, axis=-1)
        loc_s = jnp.sum(locations * mask, axis=-1).astype(jnp.int32)
        loc_oh = jax.nn.one_hot(loc_s, C, dtype=xt.dtype)
        dispatch = mask[:, :, None] * loc_oh[:, None, :]
        combine = gate[:, None, None] * dispatch
        exp_in = jnp.einsum('tec,th->ech', dispatch, xt)
        exp_out = jnp.einsum('ech,efh->ecf', exp_in, W) + b[:, None, :]
        out = jnp.einsum('tec,ecf->tf', combine, exp_out)
        return out.reshape(Bb, Ss, Hh)
    x = x + jnp.tanh(g_xattn[0]) * _L0_xattn_ref(_layernorm(x, axis=-1), ctx_1024, ctx_1024, L0_xattn_Wq, L0_xattn_bq, L0_xattn_Wk, L0_xattn_bk, L0_xattn_Wv, L0_xattn_bv, L0_xattn_Wo, L0_xattn_bo)
    x = x + jnp.tanh(g_ffn[0]) * _L0_ffn_ref(_layernorm(x, axis=-1), L0_ffn_wg, L0_ffn_W, L0_ffn_b)
    return x

_drawn_inputs = setup_inputs


def setup_inputs(seed=0):
    import zlib

    import numpy as np

    out = dict(_drawn_inputs(seed))
    spreads = {'L0_xattn_bq': (0.0, 0.469),
     'L0_xattn_bk': (0.0, 0.8),
     'L0_xattn_bv': (0.0, 0.1),
     'L0_xattn_bo': (0.0, 0.1)}
    factors = {'L0_ffn_b': 8.0}
    for name, (base, spread) in spreads.items():
        noise = np.random.default_rng([zlib.crc32(name.encode()), seed]).standard_normal(out[name].shape)
        drawn = base * np.exp(spread * noise) if base else spread * noise
        out[name] = jnp.asarray(drawn.astype(out[name].dtype))
    for name, factor in factors.items():
        out[name] = (out[name] * factor).astype(out[name].dtype)
    return out
```

```python
from contextlib import ExitStack

import concourse.bass as bass
from concourse import mybir

ALU = mybir.AluOpType
ACT = mybir.ActivationFunctionType
AX = mybir.AxisListType
F32 = mybir.dt.float32
BF16 = mybir.dt.bfloat16

P = 128
NB = 8
SEQ = 256
D = 128
H = 16
HD = D // H
TILES = SEQ // P
PAIRS = H // 2
HALF = PAIRS // 2
EXPERTS = 8
CAPACITY = NB * SEQ // EXPERTS
SLOTS = 6
HROWS = SLOTS * HD
QROWS = 2 * HROWS
KROWS = QROWS + 2
UNITS = 16
SCALE = float(HD) ** -0.5
EPS = 1e-5
DMA = 16


def build(nc, x, ctx_in, g_xattn, g_ffn, Wq, bq, Wk, bk, Wv, bv, Wo, bo, wg, W, b_exp, out):
    es = ExitStack()
    with es:
        def sb(name, shape, dt=F32):
            return es.enter_context(nc.sbuf_tensor(name, shape, dt))

        def bank(name):
            return es.enter_context(nc.psum_tensor(name, [P, 512], F32))

        def sem(name):
            return es.enter_context(nc.semaphore(name))

        q_scr = [nc.dram_tensor(f"q_scr{i}", (SLOTS, P, SEQ), BF16, kind="Internal").ap() for i in range(2)]
        k_scr = [nc.dram_tensor(f"k_scr{i}", (SLOTS, P, SEQ), BF16, kind="Internal").ap() for i in range(2)]

        ident = sb("ident", [P, P])
        identb = sb("identb", [P, P], BF16)
        before = sb("before", [P, P], BF16)
        ones = sb("ones", [P, P], BF16)
        rank = sb("rank", [P, TILES, EXPERTS])
        minus_half = sb("minus_half", [P, TILES])
        w_raw = sb("w_raw", [P, 4, D])
        we_raw = sb("we_raw", [P, EXPERTS, D])
        wqT = sb("wqT", [P, 2, HD, PAIRS])
        wkT = sb("wkT", [P, 2, HD, PAIRS])
        wvT = sb("wvT", [P, D])
        woT = sb("woT", [P, D])
        weT = sb("weT", [P, EXPERTS, D])
        wg_sb = sb("wg_sb", [P, EXPERTS])
        bq_col = sb("bq_col", [P, 1])
        bk_col = sb("bk_col", [P, 1])
        bv_row = sb("bv_row", [P, D])
        bo_row = sb("bo_row", [P, D])
        gbo_row = sb("gbo_row", [P, D])
        be_sb = sb("be_sb", [EXPERTS, D])
        gates = sb("gates", [P, 2])
        tg = sb("tg", [P, 2])

        xin = [sb(f"xin{i}", [P, TILES, D]) for i in range(2)]
        cin = [sb(f"cin{i}", [P, TILES, D]) for i in range(2)]
        xres = [sb(f"xres{i}", [P, TILES, D]) for i in range(2)]
        stat1 = sb("stat1", [P, TILES, 6])
        mv1 = sb("mv1", [P, TILES, 2])
        var1 = sb("var1", [P, TILES])
        rstd1 = sb("rstd1", [P, TILES])
        xn = sb("xn", [P, TILES, D])
        frontT = [sb(f"frontT{i}", [P, 2, SEQ]) for i in range(2)]
        qk = sb("qk", [P, 2, SEQ])
        parts = sb("parts", [P, 3, 2, SEQ], BF16)
        rest = sb("rest", [P, 2, SEQ])
        qz = [sb(f"qz{i}", [P, 2, 2, HALF, SEQ], BF16) for i in range(2)]
        kst = [sb(f"kst{i}", [P, PAIRS, SEQ], BF16) for i in range(2)]
        vaug = [sb(f"vaug{i}", [P, TILES, H, 32]) for i in range(2)]
        negmax = sb("negmax", [P, 2, TILES, 2, HALF])
        mneg = sb("mneg", [P, 2, TILES, 2, 2 * HALF], BF16)
        mT = [sb(f"mT{i}", [4 * HALF, SEQ], BF16) for i in range(2)]
        probs = sb("probs", [P, UNITS, 2, SEQ])
        o_sb = sb("o_sb", [P, 2, SEQ])
        rsum = sb("rsum", [P, TILES * HALF * 2, 2])
        attn = sb("attn", [P, TILES, D])
        attnT = sb("attnT", [P, SEQ])
        x2 = [sb(f"x2_{i}", [P, TILES, D]) for i in range(2)]
        stat2 = sb("stat2", [P, TILES, 6])
        mv2 = sb("mv2", [P, TILES, 2])
        var2 = sb("var2", [P, TILES])
        rstd2 = sb("rstd2", [P, TILES])
        x2n = sb("x2n", [P, TILES, D])
        x2T = [sb(f"x2T{i}", [P, SEQ]) for i in range(2)]
        lmax = sb("lmax", [P, TILES])
        lsub = sb("lsub", [P, TILES, EXPERTS])
        lexp = sb("lexp", [P, TILES, EXPERTS])
        lsum = sb("lsum", [P, TILES])
        lrec = sb("lrec", [P, TILES])
        score = sb("score", [P, TILES, EXPERTS])
        smax = sb("smax", [P, TILES])
        chosen = sb("chosen", [P, TILES, EXPERTS], BF16)
        counts = sb("counts", [P, EXPERTS], BF16)
        gate = [sb(f"gate{i}", [P, TILES]) for i in range(2)]
        kept = [sb(f"kept{i}", [P, TILES, EXPERTS], BF16) for i in range(2)]
        keptT = sb("keptT", [EXPERTS, SEQ])
        xm = [sb(f"xm{i}", [P, 4, P]) for i in range(2)]
        res = sb("res", [P, NB * TILES, D])

        peak_ps = [bank("peak_ps0"), bank("peak_ps1")]
        st_ps = [bank("st_ps0"), bank("st_ps1")]
        o_ps = bank("o_ps")
        work = bank("work")
        mask_ps = bank("mask_ps")
        y_ps = bank("y_ps")
        work_b = work[:, :].bitcast(BF16)

        x_in, c_in, xr_in = sem("x_in"), sem("c_in"), sem("xr_in")
        split_out = sem("split_out")
        stack_in = [sem("stack_in0"), sem("stack_in1")]
        max_in = [sem("max_in0"), sem("max_in1")]
        stored = sem("stored")
        var1_ready, rstd1_ready, xn_ready = sem("var1_ready"), sem("rstd1_ready"), sem("xn_ready")
        frontT_mm, frontT_ready = sem("frontT_mm"), sem("frontT_ready")
        qk_mm, qk_ready = sem("qk_mm"), sem("qk_ready")
        part1_ready, rest_ready = sem("part1_ready"), sem("rest_ready")
        part2_ready, part3_ready = sem("part2_ready"), sem("part3_ready")
        v_mm, v_ready = sem("v_mm"), sem("v_ready")
        peak_mm, peak_read = sem("peak_mm"), sem("peak_read")
        hi_ready, mneg_ready = sem("hi_ready"), sem("mneg_ready")
        mT_mm, mT_ready = sem("mT_mm"), sem("mT_ready")
        st_mm, exp_ready = sem("st_mm"), sem("exp_ready")
        pv_mm = sem("pv_mm")
        o_ready, oT_mm, rsum_ready, attn_ready = sem("o_ready"), sem("oT_mm"), sem("rsum_ready"), sem("attn_ready")
        attnT_mm, attnT_ready, proj_mm = sem("attnT_mm"), sem("attnT_ready"), sem("proj_mm")
        xres_ready, x2_ready = sem("xres_ready"), sem("x2_ready")
        var2_ready, rstd2_ready, x2n_ready = sem("var2_ready"), sem("rstd2_ready"), sem("x2n_ready")
        x2T_mm, x2T_ready, logit_mm = sem("x2T_mm"), sem("x2T_ready"), sem("logit_mm")
        lsub_ready, lexp_ready, chosen_ready = sem("lsub_ready"), sem("lexp_ready"), sem("chosen_ready")
        loc_mm, kept_ready = sem("loc_mm"), sem("kept_ready")
        keptT_mm, keptT_ready = sem("keptT_mm"), sem("keptT_ready")
        mask_mm, xm_ready, y_mm = sem("mask_mm"), sem("xm_ready"), sem("y_mm")
        res_ready = sem("res_ready")
        stat1_done, mv1_done = sem("stat1_done"), sem("mv1_done")
        stat2_done, mv2_done = sem("stat2_done"), sem("mv2_done")
        lmax_done, score_done, smax_done = sem("lmax_done"), sem("score_done"), sem("smax_done")
        lsum_done, lrec_done, counts_done = sem("lsum_done"), sem("lrec_done"), sem("counts_done")
        wqk_in, wvo_in, we_in, small_in = sem("wqk_in"), sem("wvo_in"), sem("we_in"), sem("small_in")
        ident_ready, const_ready, cleared = sem("ident_ready"), sem("const_ready"), sem("cleared")
        drawn = sem("drawn")
        wT_mm, wT_ready, weT_mm, weT_ready, tg_ready, gbo_ready = (
            sem("wT_mm"), sem("wT_ready"), sem("weT_mm"), sem("weT_ready"), sem("tg_ready"), sem("gbo_ready"))

        def wait(eng, s, batch, k=1, per=1, unit=1):
            if isinstance(batch, int):
                count = min(batch * per + k, NB * per)
                if count > 0:
                    eng.wait_ge(s, count * unit)
            else:
                eng.wait_ge(s, batch * (per * unit) + k * unit)

        def live(batch):
            return not isinstance(batch, int) or 0 <= batch < NB

        def steps(eng, step):
            for n in range(-2, 2):
                step(n, n % 2)
            with eng.Fori(1, NB // 2 - 1) as twice:
                step(twice * 2, 0)
                step(twice * 2 + 1, 1)
            for n in range(NB - 2, NB + 2):
                step(n, n % 2)

        block = es.enter_context(nc.Block())

        @block.sync
        def _(sp):
            x_rows = x.rearrange("b (t p) d -> p (b t) d", p=P)
            c_rows = ctx_in.rearrange("b (t p) d -> p (b t) d", p=P)
            o_rows = out.rearrange("b (t p) d -> p (b t) d", p=P)

            def rows(ap, tile):
                return ap[:, bass.ds(tile, TILES), :]

            def tile_of(batch):
                return batch * TILES if isinstance(batch, int) else sp.snap(batch * TILES)


            def load_small():
                sp.dma_start(bq_col[:], bq.rearrange("(p r d) -> r d p", r=2, d=HD), allow_slow_non_contiguous=True).then_inc(small_in, DMA)
                sp.dma_start(bk_col[:], bk.rearrange("(p r d) -> r d p", r=2, d=HD), allow_slow_non_contiguous=True).then_inc(small_in, DMA)
                sp.dma_start(bv_row[:], bv.unsqueeze(0).broadcast_to([P, D])).then_inc(small_in, DMA)
                sp.dma_start(bo_row[:], bo.unsqueeze(0).broadcast_to([P, D])).then_inc(small_in, DMA)
                sp.dma_start(gates[:, 0:1], g_xattn.unsqueeze(0).broadcast_to([P, 1])).then_inc(small_in, DMA)
                sp.dma_start(gates[:, 1:2], g_ffn.unsqueeze(0).broadcast_to([P, 1])).then_inc(small_in, DMA)
                sp.dma_start(wg_sb[:], wg).then_inc(small_in, DMA)
                sp.dma_start(be_sb[:], b_exp).then_inc(small_in, DMA)

            def load_stack(batch, par, half):
                wait(sp, st_mm, batch - 2, UNITS // 2 * (half + 1), UNITS)
                wait(sp, split_out, batch, 6, 6, DMA)
                if isinstance(batch, int) and batch < 2:
                    sp.wait_ge(cleared, 6)
                pairs = slice(half * HALF, (half + 1) * HALF)
                for r in range(2):
                    for dst, scr in ((kst[par][r * HROWS:(r + 1) * HROWS, pairs, :], k_scr[par]),
                                     (qz[par][r * HROWS:(r + 1) * HROWS, half, r, :, :], q_scr[par])):
                        src = scr.rearrange("s (r d p) q -> r s d p q", r=2, d=HD)[r, :, :, pairs, :]
                        sp.dma_start(dst, src.rearrange("s d p q -> s d (p q)")).then_inc(stack_in[half], DMA)

            def load_max(batch, par, half):
                wait(sp, mT_ready, batch, half + 1, 2)
                sp.dma_start(qz[par][QROWS:KROWS, half].rearrange("a r p q -> a (r p) q"),
                             mT[half][:]).then_inc(max_in[half], DMA)

            def step(n, cur):
                nxt = 1 - cur
                front_tile, attend_tile, expert_tile = tile_of(n + 2), tile_of(n), tile_of(n - 2)
                if live(n + 2):
                    wait(sp, xn_ready, n)
                    sp.dma_start(xin[cur][:], rows(x_rows, front_tile)).then_inc(x_in, DMA)
                    wait(sp, frontT_mm, n)
                    sp.dma_start(cin[cur][:], rows(c_rows, front_tile)).then_inc(c_in, DMA)
                if isinstance(n, int) and n == -2:
                    load_small()
                if live(n + 1):
                    load_stack(n + 1, nxt, 1)
                if live(n):
                    load_max(n, cur, 1)
                    wait(sp, x2_ready, n - 2)
                    wait(sp, xres_ready, n - 1)
                    sp.dma_start(xres[cur][:], rows(x_rows, attend_tile)).then_inc(xr_in, DMA)
                if live(n + 2):
                    for part, ready, q_slots, k_slots in (
                            (0, part1_ready, slice(0, 3), slice(1, 6, 2)),
                            (1, part2_ready, slice(3, 5), slice(2, 5, 2)),
                            (2, part3_ready, slice(5, 6), slice(0, 1))):
                        wait(sp, ready, n + 2)
                        for t, scr, slots in ((0, q_scr[cur], q_slots), (1, k_scr[cur], k_slots)):
                            dst = scr[slots].rearrange("s z q -> z s q")
                            src = parts[:, part, t, :].unsqueeze(1).broadcast_to(list(dst.shape))
                            sp.dma_start(dst, src).then_inc(split_out, DMA)
                if live(n + 1):
                    load_max(n + 1, nxt, 0)
                if live(n + 2):
                    load_stack(n + 2, cur, 0)
                if live(n - 2):
                    wait(sp, res_ready, n - 2)
                    sp.dma_start(rows(o_rows, expert_tile), rows(res[:], expert_tile)).then_inc(stored, DMA)

            steps(sp, step)
            sp.wait_ge(stored, NB * DMA)

        @block.gpsimd
        def _(pool):
            nc.gpsimd.memset(ident[:], 0.0).then_inc(drawn, 1)
            pool.wait_ge(drawn, 1)
            nc.gpsimd.affine_select(out=ident[:], in_=ident[:], compare_op=ALU.not_equal, fill=1.0, base=0,
                                    pattern=[[-1, P]], channel_multiplier=1).then_inc(ident_ready, 1)
            nc.gpsimd.memset(minus_half[:], -0.5).then_inc(ident_ready, 1)
            nc.gpsimd.memset(kst[0][:], 1.0).then_inc(cleared, 1)
            nc.gpsimd.memset(ones[:], 1.0).then_inc(drawn, 1)
            pool.wait_ge(ident_ready, 2)
            nc.gpsimd.tensor_copy(identb[:], ident[:]).then_inc(const_ready, 1)
            pool.wait_ge(drawn, 2)
            nc.gpsimd.affine_select(out=before[:], in_=ones[:], compare_op=ALU.is_gt, fill=0.0, base=0,
                                    pattern=[[1, P]], channel_multiplier=-1).then_inc(const_ready, 1)
            for e in range(EXPERTS):
                nc.gpsimd.memset(rank[:, :, e:e + 1], float(EXPERTS - e)).then_inc(const_ready, 1)

            def split(batch):
                wait(pool, part1_ready, batch)
                wait(pool, part2_ready, batch - 1)
                nc.gpsimd.tensor_tensor(rest[:], qk[:], parts[:, 0], ALU.subtract).then_inc(rest_ready, 1)
                wait(pool, part2_ready, batch)
                wait(pool, split_out, batch - 1, 6, 6, DMA)
                nc.gpsimd.tensor_tensor(parts[:, 2], rest[:], parts[:, 1], ALU.subtract).then_inc(part3_ready, 1)

            def step(n, cur):
                nxt = 1 - cur
                if live(n - 1):
                    wait(pool, xr_in, n - 1, 1, 1, DMA)
                    if isinstance(n, int):
                        pool.wait_ge(gbo_ready, 1)
                    nc.gpsimd.tensor_tensor(xres[nxt][:], xres[nxt][:],
                                            gbo_row[:].unsqueeze(1).broadcast_to([P, TILES, D]),
                                            ALU.add).then_inc(xres_ready, 1)
                if live(n + 2):
                    wait(pool, var1_ready, n + 2)
                    nc.gpsimd.tensor_tensor(rstd1[:], var1[:], minus_half[:], ALU.pow).then_inc(rstd1_ready, 1)
                if live(n - 1):
                    wait(pool, var2_ready, n - 1)
                    nc.gpsimd.tensor_tensor(rstd2[:], var2[:], minus_half[:], ALU.pow).then_inc(rstd2_ready, 1)
                if live(n + 2):
                    split(n + 2)

            steps(pool, step)

        @block.scalar
        def _(act):
            act.dma_start(w_raw[:, 0], Wq).then_inc(wqk_in, DMA)
            act.dma_start(w_raw[:, 1], Wk).then_inc(wqk_in, DMA)
            act.dma_start(w_raw[:, 2], Wv).then_inc(wvo_in, DMA)
            act.dma_start(w_raw[:, 3], Wo).then_inc(wvo_in, DMA)
            act.dma_start(we_raw[:], W.rearrange("e f h -> f e h")).then_inc(we_in, DMA)
            act.wait_ge(wT_mm, 2)
            nc.scalar.copy(wqT[:], work[:, 0:D].rearrange("z (p r d) -> z r d p", r=2, d=HD)).then_inc(wT_ready, 1)
            nc.scalar.copy(wkT[:], work[:, D:2 * D].rearrange("z (p r d) -> z r d p", r=2, d=HD)).then_inc(wT_ready, 1)
            act.wait_ge(small_in, 8 * DMA)

            def late_setup():
                nc.scalar.activation(tg[:], gates[:], ACT.Tanh).then_inc(tg_ready, 1)
                act.wait_ge(wT_mm, 4)
                nc.scalar.copy(wvT[:], y_ps[:, 0:D]).then_inc(wT_ready, 1)
                nc.scalar.copy(woT[:], y_ps[:, D:2 * D]).then_inc(wT_ready, 1)
                for half in range(2):
                    act.wait_ge(weT_mm, half + 1)
                    nc.scalar.copy(weT[:, 4 * half:4 * half + 4, :], st_ps[half][:]).then_inc(weT_ready, 1)

            def copy_max(batch, half):
                wait(act, mT_mm, batch, half + 1, 2)
                wait(act, max_in[half], batch - 1, 1, 1, DMA)
                nc.scalar.copy(mT[half][:], work_b[0:4 * HALF, 0:SEQ]).then_inc(mT_ready, 1)

            def step(n, cur):
                nxt = 1 - cur
                for s in range(UNITS):
                    if live(n):
                        wait(act, st_mm, n, s + 1, UNITS)
                        wait(act, pv_mm, n - 1, s // 4 + 1, 4)
                        nc.scalar.activation(probs[:, s], st_ps[s % 2][:], ACT.Exp,
                                             scale=SCALE).then_inc(exp_ready, 1)
                    if s == 1:
                        if live(n - 1):
                            wait(act, pv_mm, n - 1, 4, 4)
                            wait(act, oT_mm, n - 2)
                            nc.scalar.copy(o_sb[:], o_ps[:]).then_inc(o_ready, 1)
                        if live(n - 2):
                            wait(act, keptT_mm, n - 2)
                        if live(n):
                            copy_max(n, 1)
                        if live(n - 2):
                            nc.scalar.copy(keptT[:], work_b[0:EXPERTS, SEQ:2 * SEQ]).then_inc(keptT_ready, 1)
                    if s == 4 and live(n - 1):
                        wait(act, attnT_mm, n - 1)
                        nc.scalar.copy(attnT[:], work[:, 0:SEQ]).then_inc(attnT_ready, 1)
                    if s == 5 and live(n + 2):
                        wait(act, frontT_mm, n + 2)
                        nc.scalar.copy(frontT[cur][:], work[:]).then_inc(frontT_ready, 1)
                    if s == 7 and live(n + 2):
                        wait(act, qk_mm, n + 2)
                        wait(act, rest_ready, n + 1)
                        for t, bias in ((0, bq_col), (1, bk_col)):
                            last = nc.scalar.activation(qk[:, t], work[:, t * SEQ:(t + 1) * SEQ], ACT.Identity,
                                                        bias=bias[:, 0:1])
                        last.then_inc(qk_ready, 1)
                    if s == 9 and live(n + 1):
                        copy_max(n + 1, 0)
                    if s == 10 and live(n - 1):
                        wait(act, x2T_mm, n - 1)
                        nc.scalar.copy(x2T[nxt][:], work[:, 0:SEQ]).then_inc(x2T_ready, 1)
                    if s == 13 and live(n - 1):
                        wait(act, lsub_ready, n - 1)
                        nc.scalar.activation(lexp[:], lsub[:], ACT.Exp).then_inc(lexp_ready, 1)
                if isinstance(n, int) and n == -2:
                    late_setup()

            steps(act, step)

        @block.vector
        def _(dve):
            def peak(batch, s):
                half, p, r = s // 8, (s % 8) // 2, s % 2
                wait(dve, peak_mm, batch, s + 1, UNITS)
                nc.vector.tensor_reduce(negmax[:, half, :, r, p], peak_ps[s % 2][:].rearrange("z (t k) -> z t k", t=TILES),
                                        axis=AX.X, op=ALU.max, negate=True).then_inc(peak_read, 1)

            def split_max(batch, half):
                src = negmax[:, half].rearrange("z t r p -> z t (r p)")
                wait(dve, peak_read, batch, 8 * (half + 1), UNITS)
                nc.vector.tensor_copy(mneg[:, half, :, 0, :], src).then_inc(hi_ready, 1)
                wait(dve, hi_ready, batch, half + 1, 2)
                nc.vector.tensor_tensor(mneg[:, half, :, 1, :], src, mneg[:, half, :, 0, :],
                                        ALU.subtract).then_inc(mneg_ready, 1)

            def statistics(src, stat, stat_done):
                for t in range(TILES):
                    last = nc.vector.bn_stats(stat[:, t], src[:, t])
                last.then_inc(stat_done, 1)

            def variance(batch, stat, mv, var, mv_done, var_ready):
                for t in range(TILES):
                    last = nc.vector.bn_aggr(mv[:, t], stat[:, t])
                last.then_inc(mv_done, 1)
                wait(dve, mv_done, batch)
                nc.vector.tensor_scalar(var[:], mv[:, :, 1], EPS, None, ALU.add).then_inc(var_ready, 1)

            def norm(dst, src, mv, rstd, ready):
                for t in range(TILES):
                    last = nc.vector.tensor_scalar(dst[:, t], src[:, t], mv[:, t, 0:1], rstd[:, t:t + 1],
                                                   ALU.subtract, ALU.mult)
                last.then_inc(ready, 1)

            def front_norm(batch, par):
                wait(dve, rstd1_ready, batch)
                wait(dve, frontT_mm, batch - 1)
                norm(xn, xin[par], mv1, rstd1, xn_ready)

            def first_part(batch):
                wait(dve, qk_ready, batch)
                wait(dve, split_out, batch - 1, 6, 6, DMA)
                nc.vector.tensor_copy(parts[:, 0], qk[:]).then_inc(part1_ready, 1)

            def second_part(batch):
                wait(dve, rest_ready, batch)
                nc.vector.tensor_copy(parts[:, 1], rest[:]).then_inc(part2_ready, 1)

            def place_v(batch, par):
                wait(dve, v_mm, batch)
                wait(dve, pv_mm, batch - 2, 4, 4)
                for t in range(TILES):
                    dst = vaug[par][:, t].rearrange("z (p r) c -> z p (r c)", r=2)
                    for r in range(2):
                        last = nc.vector.tensor_tensor(
                            dst[:, :, r * (32 + HD):r * (32 + HD) + HD],
                            work[:, t * D:(t + 1) * D].rearrange("z (p r d) -> z r p d", r=2, d=HD)[:, r],
                            bv_row[:].rearrange("z (p r d) -> z r p d", r=2, d=HD)[:, r], ALU.add)
                last.then_inc(v_ready, 1)

            def normalise(batch):
                wait(dve, oT_mm, batch)
                oT = work[:].rearrange("z (g c) -> z g c", c=32)
                nc.vector.reciprocal(rsum[:], oT[:, :, 2 * HD:2 * HD + 2]).then_inc(rsum_ready, 1)
                wait(dve, rsum_ready, batch)
                wait(dve, attnT_mm, batch - 1)
                nc.vector.tensor_tensor(
                    attn[:].rearrange("z t (g r d) -> z (t g) r d", r=2, d=HD),
                    oT[:, :, 0:2 * HD].rearrange("z g (r d) -> z g r d", r=2),
                    rsum[:].unsqueeze(3).broadcast_to([P, TILES * PAIRS, 2, HD]), ALU.mult).then_inc(attn_ready, 1)

            def residual(batch, par):
                wait(dve, proj_mm, batch)
                wait(dve, xres_ready, batch)
                nc.vector.scalar_tensor_tensor(x2[par][:].rearrange("z t d -> z (t d)"), work[:, 0:SEQ], tg[:, 0:1],
                                               xres[par][:].rearrange("z t d -> z (t d)"),
                                               ALU.mult, ALU.add).then_inc(x2_ready, 1)
                wait(dve, x2_ready, batch)
                statistics(x2[par], stat2, stat2_done)

            def choose(batch):
                wait(dve, logit_mm, batch)
                logits = work[:, 0:TILES * EXPERTS].rearrange("z (t e) -> z t e", t=TILES)
                nc.vector.tensor_reduce(lmax[:], logits, axis=AX.X, op=ALU.max).then_inc(lmax_done, 1)
                wait(dve, lmax_done, batch)
                nc.vector.tensor_tensor(lsub[:], logits, lmax[:].unsqueeze(2).broadcast_to([P, TILES, EXPERTS]),
                                        ALU.subtract).then_inc(lsub_ready, 1)
                wait(dve, lsub_ready, batch)
                nc.vector.scalar_tensor_tensor(score[:], lsub[:], 0.0, rank[:], ALU.is_ge, ALU.mult).then_inc(score_done, 1)
                wait(dve, score_done, batch)
                nc.vector.tensor_reduce(smax[:], score[:], axis=AX.X, op=ALU.max).then_inc(smax_done, 1)
                wait(dve, smax_done, batch)
                nc.vector.tensor_tensor(chosen[:], score[:], smax[:].unsqueeze(2).broadcast_to([P, TILES, EXPERTS]),
                                        ALU.is_equal).then_inc(chosen_ready, 1)

            def weigh(batch, par):
                wait(dve, lexp_ready, batch)
                nc.vector.tensor_reduce(lsum[:], lexp[:], axis=AX.X, op=ALU.add).then_inc(lsum_done, 1)
                wait(dve, lsum_done, batch)
                nc.vector.reciprocal(lrec[:], lsum[:]).then_inc(lrec_done, 1)
                wait(dve, lrec_done, batch)
                nc.vector.tensor_scalar(gate[par][:], lrec[:], tg[:, 1:2], None, ALU.mult)

            def keep(batch, par):
                wait(dve, loc_mm, batch)
                loc = work[:, 0:TILES * EXPERTS].rearrange("z (t e) -> z t e", t=TILES)
                nc.vector.scalar_tensor_tensor(kept[par][:], loc, float(CAPACITY), chosen[:],
                                               ALU.is_lt, ALU.mult).then_inc(kept_ready, 1)
                for t in range(TILES):
                    nc.vector.tensor_tensor(counts[:], counts[:], chosen[:, t], ALU.add).then_inc(counts_done, 1)
                    wait(dve, counts_done, batch, t + 1, TILES)

            def mask(batch, par, r):
                wait(dve, mask_mm, batch, r + 1, 4)
                if r >= 2:
                    wait(dve, y_mm, batch, r - 1, 4)
                t = r // 2
                nc.vector.tensor_tensor(xm[r % 2][:], mask_ps[:].rearrange("z (e k) -> z e k", e=4),
                                        x2T[par][:, t * P:(t + 1) * P].unsqueeze(1).broadcast_to([P, 4, P]),
                                        ALU.mult).then_inc(xm_ready, 1)

            def finish(batch, par):
                wait(dve, y_mm, batch, 4, 4)
                dst = res[:, bass.ds(batch * TILES, TILES), :]
                for t in range(TILES):
                    last = nc.vector.scalar_tensor_tensor(dst[:, t], y_ps[:, t * D:(t + 1) * D],
                                                          gate[par][:, t:t + 1], x2[par][:, t], ALU.mult, ALU.add)
                last.then_inc(res_ready, 1)

            def setup():
                for i in range(2):
                    nc.vector.memset(vaug[i][:], 0.0).then_inc(cleared, 1)
                    nc.vector.memset(qz[i][:].rearrange("z h r p q -> z (h r p q)").bitcast(mybir.dt.uint32), 0).then_inc(cleared, 1)
                nc.vector.memset(kst[1][:], 1.0).then_inc(cleared, 1)
                dve.wait_ge(cleared, 6)
                for i in range(2):
                    frame = vaug[i][:].rearrange("z t (p r) c -> z t p (r c)", r=2)
                    for r in range(2):
                        column = r * 32 + 2 * HD + r
                        nc.vector.memset(frame[:, :, :, column:column + 1], 1.0)
                nc.vector.memset(counts[:], 0.0)
                dve.wait_ge(small_in, 8 * DMA)
                dve.wait_ge(tg_ready, 1)
                nc.vector.tensor_scalar(gbo_row[:], bo_row[:], tg[:, 0:1], None, ALU.mult).then_inc(gbo_ready, 1)

            def step(n, cur):
                nxt = 1 - cur
                if live(n):
                    split_max(n, 1)
                if live(n + 2):
                    wait(dve, x_in, n + 2, 1, 1, DMA)
                    statistics(xin[cur], stat1, stat1_done)
                    wait(dve, stat1_done, n + 2)
                for s in range(UNITS):
                    if live(n - 2) and s in (2, 4, 7, 10):
                        mask(n - 2, cur, (2, 4, 7, 10).index(s))
                    if s == 7 and live(n - 1):
                        wait(dve, stat2_done, n - 1)
                    if live(n + 1):
                        peak(n + 1, s)
                    if s == 0 and live(n + 2):
                        variance(n + 2, stat1, mv1, var1, mv1_done, var1_ready)
                    if s == 7 and live(n - 1):
                        variance(n - 1, stat2, mv2, var2, mv2_done, var2_ready)
                    if s == 2 and live(n - 1):
                        normalise(n - 1)
                    if s == 3 and live(n + 2):
                        front_norm(n + 2, cur)
                    if s == 6 and live(n - 1):
                        residual(n - 1, nxt)
                    if s == 7 and live(n + 2):
                        first_part(n + 2)
                    if s == 7 and live(n + 1):
                        split_max(n + 1, 0)
                    if s == 9 and live(n - 1):
                        wait(dve, rstd2_ready, n - 1)
                        wait(dve, x2T_mm, n - 2)
                        norm(x2n, x2[nxt], mv2, rstd2, x2n_ready)
                    if s == 9 and live(n + 2):
                        second_part(n + 2)
                    if s == 11 and live(n + 1):
                        place_v(n + 1, nxt)
                    if s == 12 and live(n - 1):
                        choose(n - 1)
                    if s == 13 and live(n - 2):
                        finish(n - 2, cur)
                    if s == 14 and live(n - 1):
                        weigh(n - 1, nxt)
                        keep(n - 1, nxt)
                if isinstance(n, int) and n == -2:
                    setup()

            steps(dve, step)

        @block.tensor
        def _(pe):
            def turn_weights(pairs, ready):
                for dst, src in pairs:
                    last = nc.tensor.transpose(dst, src, ident[:])
                last.then_inc(ready, 1)

            pe.wait_ge(ident_ready, 1)
            pe.wait_ge(wqk_in, 2 * DMA)
            turn_weights([(work[:, 0:D], w_raw[:, 0])], wT_mm)
            turn_weights([(work[:, D:2 * D], w_raw[:, 1])], wT_mm)
            pe.wait_ge(wT_ready, 2)

            def late_setup():
                pe.wait_ge(wvo_in, 2 * DMA)
                turn_weights([(y_ps[:, 0:D], w_raw[:, 2])], wT_mm)
                turn_weights([(y_ps[:, D:2 * D], w_raw[:, 3])], wT_mm)
                pe.wait_ge(we_in, DMA)
                for half in range(2):
                    turn_weights([(st_ps[half][:, i * D:(i + 1) * D], we_raw[:, 4 * half + i]) for i in range(4)], weT_mm)
                pe.wait_ge(wT_ready, 4)
                pe.wait_ge(weT_ready, 2)
                pe.wait_ge(const_ready, 10)
                pe.wait_ge(small_in, 8 * DMA)

            def peak(batch, par, s):
                half, p, r = s // 8, s // 2, s % 2
                if s % 8 == 0:
                    wait(pe, stack_in[half], batch, 4, 4, DMA)
                wait(pe, peak_read, batch, s - 1, UNITS)
                for t in range(TILES):
                    last = nc.tensor.matmul(peak_ps[s % 2][:, t * SEQ:(t + 1) * SEQ],
                                            qz[par][0:QROWS, half, r, p % HALF, t * P:(t + 1) * P], kst[par][0:QROWS, p, :],
                                            start=True, stop=True)
                last.then_inc(peak_mm, 1)

            def scores(batch, par, s):
                half, t, g = s // 8, (s % 8) // 4, s % 4
                p = half * HALF + g
                if s % 8 == 0:
                    wait(pe, max_in[half], batch, 1, 1, DMA)
                wait(pe, exp_ready, batch, s - 1, UNITS)
                nc.tensor.matmul(st_ps[s % 2][:], kst[par][0:KROWS, p, t * P:(t + 1) * P], qz[par][0:KROWS, half, :, g, :],
                                 start=True, stop=True).then_inc(st_mm, 1)

            def values(batch, par, quarter):
                half, t = quarter // 2, quarter % 2
                wait(pe, exp_ready, batch, 4 * quarter + 4, UNITS)
                if quarter == 0:
                    wait(pe, v_ready, batch)
                    wait(pe, o_ready, batch - 1)
                for r in range(2):
                    for g in range(4):
                        last = nc.tensor.matmul(o_ps[32 * g:32 * g + 32, half * SEQ:(half + 1) * SEQ],
                                                vaug[par][:, t, 2 * (half * HALF + g) + r, :],
                                                probs[:, 4 * quarter + g, r, :],
                                                start=(t == 0 and r == 0), stop=(t == 1 and r == 1))
                last.then_inc(pv_mm, 1)

            def turn_max(batch, half):
                wait(pe, mneg_ready, batch, half + 1, 2)
                for t in range(TILES):
                    last = nc.tensor.transpose(work_b[0:4 * HALF, t * P:(t + 1) * P],
                                               mneg[:, half, t].rearrange("z a h -> z (a h)"), identb[:])
                last.then_inc(mT_mm, 1)

            def turn_kept(batch, par):
                wait(pe, kept_ready, batch)
                for t in range(TILES):
                    last = nc.tensor.transpose(work_b[0:EXPERTS, SEQ + t * P:SEQ + (t + 1) * P], kept[par][:, t], identb[:])
                last.then_inc(keptT_mm, 1)

            def spread(batch, par, r):
                t = r // 2
                if r > 0:
                    wait(pe, xm_ready, batch, r, 4)
                for i in range(4):
                    e = 4 * (r % 2) + i
                    last = nc.tensor.matmul(mask_ps[:, i * P:(i + 1) * P],
                                            kept[par][:, t, e:e + 1].broadcast_to([P, P]), identb[:],
                                            start=True, stop=True)
                last.then_inc(mask_mm, 1)

            def expert(batch, r):
                t = r // 2
                dst = y_ps[:, t * D:(t + 1) * D]
                if r == 0:
                    wait(pe, keptT_ready, batch)
                if r % 2 == 0:
                    nc.tensor.matmul(dst, keptT[:, t * P:(t + 1) * P], be_sb[:], start=True, stop=False)
                wait(pe, xm_ready, batch, r + 1, 4)
                for i in range(4):
                    last = nc.tensor.matmul(dst, xm[r % 2][:, i], weT[:, 4 * (r % 2) + i],
                                            start=False, stop=(r % 2 == 1 and i == 3))
                last.then_inc(y_mm, 1)

            def turn_front(batch, par):
                wait(pe, attnT_ready, batch - 3)
                wait(pe, qk_ready, batch - 1)
                wait(pe, xn_ready, batch)
                wait(pe, c_in, batch, 1, 1, DMA)
                for i, src in ((0, xn), (1, cin[par])):
                    for t in range(TILES):
                        last = nc.tensor.transpose(work[:, i * SEQ + t * P:i * SEQ + (t + 1) * P], src[:, t], ident[:])
                last.then_inc(frontT_mm, 1)

            def project_qk(batch, par):
                wait(pe, frontT_ready, batch)
                wait(pe, x2_ready, batch - 3)
                for i, w in ((0, wqT), (1, wkT)):
                    last = nc.tensor.matmul(work[:, i * SEQ:(i + 1) * SEQ], w[:].rearrange("z r d p -> z (r d p)"),
                                            frontT[par][:, i], start=True, stop=True)
                last.then_inc(qk_mm, 1)

            def project_v(batch, par):
                wait(pe, x2T_ready, batch - 2)
                wait(pe, mT_ready, batch, 1, 2)
                for t in range(TILES):
                    last = nc.tensor.matmul(work[:, t * D:(t + 1) * D], frontT[par][:, 1, t * P:(t + 1) * P], wvT[:],
                                            start=True, stop=True)
                last.then_inc(v_mm, 1)

            def turn_o(batch):
                wait(pe, o_ready, batch)
                wait(pe, mT_ready, batch + 1, 2, 2)
                wait(pe, keptT_ready, batch - 1)
                for t in range(TILES):
                    for half in range(2):
                        last = nc.tensor.transpose(work[:, (t * 2 + half) * P:(t * 2 + half + 1) * P],
                                                   o_sb[:, half, t * P:(t + 1) * P], ident[:])
                last.then_inc(oT_mm, 1)

            def turn_attn(batch):
                wait(pe, attn_ready, batch)
                for t in range(TILES):
                    last = nc.tensor.transpose(work[:, t * P:(t + 1) * P], attn[:, t], ident[:])
                last.then_inc(attnT_mm, 1)

            def project_o(batch):
                wait(pe, attnT_ready, batch)
                wait(pe, frontT_ready, batch + 3)
                for t in range(TILES):
                    last = nc.tensor.matmul(work[:, t * D:(t + 1) * D], attnT[:, t * P:(t + 1) * P], woT[:],
                                            start=True, stop=True)
                last.then_inc(proj_mm, 1)

            def turn_x2(batch):
                wait(pe, x2n_ready, batch)
                wait(pe, mT_ready, batch + 2, 1, 2)
                for t in range(TILES):
                    last = nc.tensor.transpose(work[:, t * P:(t + 1) * P], x2n[:, t], ident[:])
                last.then_inc(x2T_mm, 1)

            def route(batch, par):
                wait(pe, x2T_ready, batch)
                wait(pe, v_ready, batch + 2)
                for t in range(TILES):
                    last = nc.tensor.matmul(work[:, t * EXPERTS:(t + 1) * EXPERTS], x2T[par][:, t * P:(t + 1) * P],
                                            wg_sb[:], start=True, stop=True)
                last.then_inc(logit_mm, 1)

            def locate(batch):
                wait(pe, chosen_ready, batch)
                wait(pe, counts_done, batch - 1, 2, 2)
                for t in range(TILES):
                    dst = work[:, t * EXPERTS:(t + 1) * EXPERTS]
                    nc.tensor.matmul(dst, before[:], chosen[:, t], start=True, stop=False)
                    if t == 1:
                        nc.tensor.matmul(dst, ones[:], chosen[:, 0], start=False, stop=False)
                    last = nc.tensor.matmul(dst, ones[:], counts[:], start=False, stop=True)
                last.then_inc(loc_mm, 1)

            def step(n, cur):
                nxt = 1 - cur
                for s in range(UNITS):
                    if live(n + 1):
                        peak(n + 1, nxt, s)
                    if live(n):
                        scores(n, cur, s)
                    if s == 0 and live(n - 1):
                        values(n - 1, nxt, 3)
                    if s in (4, 8, 12) and live(n):
                        values(n, cur, s // 4 - 1)
                    if s == 1:
                        if live(n):
                            wait(pe, kept_ready, n - 2)
                            wait(pe, v_ready, n)
                            turn_max(n, 1)
                        if live(n - 2):
                            turn_kept(n - 2, cur)
                    if live(n - 2):
                        if s in (3, 6, 9, 13):
                            expert(n - 2, (3, 6, 9, 13).index(s))
                        if s in (1, 3, 6, 9):
                            spread(n - 2, cur, (1, 3, 6, 9).index(s))
                    if s == 2 and live(n - 1):
                        turn_o(n - 1)
                    if s == 4 and live(n - 1):
                        turn_attn(n - 1)
                    if s == 5 and live(n + 2):
                        turn_front(n + 2, cur)
                    if s == 6 and live(n - 1):
                        project_o(n - 1)
                    if s == 7 and live(n + 2):
                        project_qk(n + 2, cur)
                    if s == 9 and live(n + 1):
                        wait(pe, qk_ready, n + 2)
                        wait(pe, x2_ready, n - 1)
                        turn_max(n + 1, 0)
                    if s == 10 and live(n - 1):
                        turn_x2(n - 1)
                    if s == 11 and live(n + 1):
                        project_v(n + 1, nxt)
                    if s == 12 and live(n - 1):
                        route(n - 1, nxt)
                    if s == 14 and live(n - 1):
                        locate(n - 1)
                if isinstance(n, int) and n == -2:
                    late_setup()

            steps(pe, step)


_INS = ['x', 'ctx_1024', 'g_xattn', 'g_ffn', 'L0_xattn_Wq', 'L0_xattn_bq', 'L0_xattn_Wk', 'L0_xattn_bk',
        'L0_xattn_Wv', 'L0_xattn_bv', 'L0_xattn_Wo', 'L0_xattn_bo', 'L0_ffn_wg', 'L0_ffn_W', 'L0_ffn_b']


def kernel(**inputs):
    import numpy as _np
    import concourse.bacc as _bacc
    from concourse.bass_utils import run_bass_kernel_spmd as _run

    nc = _bacc.Bacc("TRN2", target_bir_lowering=False, num_devices=1)
    arrays, args = {}, []
    for name in _INS:
        a = _np.ascontiguousarray(inputs[name])
        arrays[f"in_{name}"] = a
        args.append(nc.dram_tensor(f"in_{name}", a.shape, mybir.dt.from_np(a.dtype), kind="ExternalInput").ap())
    o = nc.dram_tensor("out_0", (NB, SEQ, D), F32, kind="ExternalOutput").ap()
    build(nc, *args, o)
    r = _run(nc, [arrays], core_ids=[0])
    return r.results[0]["out_0"]
```

```python
from contextlib import ExitStack

import concourse.bass as bass
from concourse import mybir

ALU = mybir.AluOpType
ACT = mybir.ActivationFunctionType
AX = mybir.AxisListType
F32 = mybir.dt.float32
BF16 = mybir.dt.bfloat16

P = 128
NB = 8
SEQ = 256
D = 128
H = 16
HD = D // H
TILES = SEQ // P
PAIRS = H // 2
HALF = PAIRS // 2
EXPERTS = 8
CAPACITY = NB * SEQ // EXPERTS
SLOTS = 6
HROWS = SLOTS * HD
QROWS = 2 * HROWS
KROWS = QROWS + 2
UNITS = 16
SCALE = float(HD) ** -0.5
EPS = 1e-5
VALUES_AT = (5, 10, 14)
EXPERT_AT = (7, 9, 11, 13)
DMA = 16


def build(nc, x, ctx_in, g_xattn, g_ffn, Wq, bq, Wk, bk, Wv, bv, Wo, bo, wg, W, b_exp, out):
    es = ExitStack()
    with es:
        def sb(name, shape, dt=F32):
            return es.enter_context(nc.sbuf_tensor(name, shape, dt))

        def bank(name):
            return es.enter_context(nc.psum_tensor(name, [P, 512], F32))

        def sem(name):
            return es.enter_context(nc.semaphore(name))

        q_scr = [nc.dram_tensor(f"q_scr{i}", (SLOTS, P, SEQ), BF16, kind="Internal").ap() for i in range(2)]
        k_scr = [nc.dram_tensor(f"k_scr{i}", (SLOTS, P, SEQ), BF16, kind="Internal").ap() for i in range(2)]

        ident = sb("ident", [P, P])
        identb = sb("identb", [P, P], BF16)
        before = sb("before", [P, P], BF16)
        ones = sb("ones", [P, P], BF16)
        rank = sb("rank", [P, TILES, EXPERTS])
        minus_half = sb("minus_half", [P, TILES])
        w_raw = sb("w_raw", [P, 4, D])
        we_raw = sb("we_raw", [P, EXPERTS, D])
        wqT = sb("wqT", [P, 2, HD, PAIRS])
        wkT = sb("wkT", [P, 2, HD, PAIRS])
        wvT = sb("wvT", [P, D])
        woT = sb("woT", [P, D])
        weT = sb("weT", [P, EXPERTS, D])
        wg_sb = sb("wg_sb", [P, EXPERTS])
        bq_col = sb("bq_col", [P, 1])
        bk_col = sb("bk_col", [P, 1])
        bv_row = sb("bv_row", [P, D])
        bo_row = sb("bo_row", [P, D])
        gbo_row = sb("gbo_row", [P, D])
        be_sb = sb("be_sb", [EXPERTS, D])
        gates = sb("gates", [P, 2])
        warm = sb("warm", [P, 1])
        tg = sb("tg", [P, 2])

        xin = [sb(f"xin{i}", [P, TILES, D]) for i in range(2)]
        cin = [sb(f"cin{i}", [P, TILES, D]) for i in range(2)]
        xres = [sb(f"xres{i}", [P, TILES, D]) for i in range(2)]
        stat1 = sb("stat1", [P, TILES, 6])
        mv1 = sb("mv1", [P, TILES, 2])
        var1 = sb("var1", [P, TILES])
        rstd1 = sb("rstd1", [P, TILES])
        xn = sb("xn", [P, TILES, D])
        frontT = [sb(f"frontT{i}", [P, 2, SEQ]) for i in range(2)]
        qk = sb("qk", [P, 2, SEQ])
        parts = sb("parts", [P, 3, 2, SEQ], BF16)
        rest = sb("rest", [P, 2, SEQ])
        qz = [sb(f"qz{i}", [P, 2, 2, HALF, SEQ], BF16) for i in range(2)]
        kst = [sb(f"kst{i}", [P, PAIRS, SEQ], BF16) for i in range(2)]
        vaug = [sb(f"vaug{i}", [P, TILES, H, 32]) for i in range(2)]
        negmax = sb("negmax", [P, 2, TILES, 2, HALF])
        mneg = sb("mneg", [P, 2, TILES, 2, 2 * HALF], BF16)
        mT = [sb(f"mT{i}", [4 * HALF, SEQ], BF16) for i in range(2)]
        probs = sb("probs", [P, UNITS, 2, SEQ])
        o_sb = sb("o_sb", [P, 2, SEQ])
        rsum = sb("rsum", [P, TILES * HALF * 2, 2])
        attn = sb("attn", [P, TILES, D])
        attnT = sb("attnT", [P, SEQ])
        x2 = [sb(f"x2_{i}", [P, TILES, D]) for i in range(2)]
        stat2 = sb("stat2", [P, TILES, 6])
        mv2 = sb("mv2", [P, TILES, 2])
        var2 = sb("var2", [P, TILES])
        rstd2 = sb("rstd2", [P, TILES])
        x2n = sb("x2n", [P, TILES, D])
        x2T = [sb(f"x2T{i}", [P, SEQ]) for i in range(2)]
        lmax = sb("lmax", [P, TILES])
        lsub = sb("lsub", [P, TILES, EXPERTS])
        lexp = sb("lexp", [P, TILES, EXPERTS])
        lsum = sb("lsum", [P, TILES])
        lrec = sb("lrec", [P, TILES])
        score = sb("score", [P, TILES, EXPERTS])
        smax = sb("smax", [P, TILES])
        chosen = sb("chosen", [P, TILES, EXPERTS], BF16)
        counts = sb("counts", [P, EXPERTS], BF16)
        gate = sb("gate", [P, TILES])
        kept = sb("kept", [P, TILES, EXPERTS])
        share = sb("share", [P, TILES, EXPERTS])
        shareT = sb("shareT", [EXPERTS, SEQ])
        scaled = [sb(f"scaled{t}", [P, EXPERTS, D]) for t in range(TILES)]
        fold2, fold1 = sb("fold2", [P, 2, D]), sb("fold1", [P, D])
        first_sum = sb("first_sum", [P, TILES, D])
        tail4, tail2, tail1 = sb("tail4", [P, 4, D]), sb("tail2", [P, 2, D]), sb("tail1", [P, 1, D])
        base = sb("base", [P, TILES, D])
        res = sb("res", [P, NB * TILES, D])

        peak_ps = [bank("peak_ps0"), bank("peak_ps1")]
        st_ps = [bank("st_ps0"), bank("st_ps1")]
        o_ps = bank("o_ps")
        front_ps = bank("front_ps")
        post_ps = bank("post_ps")
        y_ps = bank("y_ps")
        front_b = front_ps[:, :].bitcast(BF16)

        x_in, c_in = [sem("x_in0"), sem("x_in1")], [sem("c_in0"), sem("c_in1")]
        xr_in = sem("xr_in")
        split_out = sem("split_out")
        stack_in = [sem("stack_in0"), sem("stack_in1")]
        max_in = [sem("max_in0"), sem("max_in1")]
        stored = sem("stored")
        var1_ready, rstd1_ready, xn_ready = sem("var1_ready"), sem("rstd1_ready"), sem("xn_ready")
        frontT_mm, frontT_ready = sem("frontT_mm"), sem("frontT_ready")
        qk_mm, qk_ready = sem("qk_mm"), sem("qk_ready")
        part1_ready, rest_ready = sem("part1_ready"), sem("rest_ready")
        part2_ready, part3_ready = sem("part2_ready"), sem("part3_ready")
        v_mm, v_ready = sem("v_mm"), sem("v_ready")
        peak_mm, peak_read = sem("peak_mm"), sem("peak_read")
        hi_ready, mneg_ready = sem("hi_ready"), sem("mneg_ready")
        mT_mm, mT_ready = sem("mT_mm"), sem("mT_ready")
        st_mm, exp_ready = sem("st_mm"), sem("exp_ready")
        pv_mm = sem("pv_mm")
        o_ready, oT_mm, rsum_ready, attn_ready = sem("o_ready"), sem("oT_mm"), sem("rsum_ready"), sem("attn_ready")
        attnT_mm, attnT_ready, proj_mm = sem("attnT_mm"), sem("attnT_ready"), sem("proj_mm")
        xres_ready, x2_ready = sem("xres_ready"), sem("x2_ready")
        var2_ready, rstd2_ready, x2n_ready = sem("var2_ready"), sem("rstd2_ready"), sem("x2n_ready")
        x2T_mm, x2T_ready, logit_mm = sem("x2T_mm"), sem("x2T_ready"), sem("logit_mm")
        lsub_ready, lexp_ready, chosen_ready = sem("lsub_ready"), sem("lexp_ready"), sem("chosen_ready")
        gate_ready, loc_mm, kept_ready, share_ready = sem("gate_ready"), sem("loc_mm"), sem("kept_ready"), sem("share_ready")
        shareT_mm, shareT_ready = sem("shareT_mm"), sem("shareT_ready")
        bias_mm, base_ready, y_mm, scaled_ready = sem("bias_mm"), sem("base_ready"), sem("y_mm"), sem("scaled_ready")
        folded, first_half = sem("folded"), sem("first_half")
        res_ready = sem("res_ready")
        stat1_done, mv1_done = sem("stat1_done"), sem("mv1_done")
        stat2_done, mv2_done = sem("stat2_done"), sem("mv2_done")
        lmax_done, score_done, smax_done = sem("lmax_done"), sem("score_done"), sem("smax_done")
        lsum_done, lrec_done, counts_done = sem("lsum_done"), sem("lrec_done"), sem("counts_done")
        tail = sem("tail")
        wqk_in, wvo_in, we_in, small_in = sem("wqk_in"), sem("wvo_in"), sem("we_in"), sem("small_in")
        bias_in = sem("bias_in")
        ident_ready, const_ready, cleared, framed = sem("ident_ready"), sem("const_ready"), sem("cleared"), sem("framed")
        drawn = sem("drawn")
        wT_mm, wT_ready, weT_mm, weT_ready, tg_ready, gbo_ready = (
            sem("wT_mm"), sem("wT_ready"), sem("weT_mm"), sem("weT_ready"), sem("tg_ready"), sem("gbo_ready"))

        def wait(eng, s, batch, k=1, per=1, unit=1):
            if isinstance(batch, int):
                count = min(batch * per + k, NB * per)
                if count > 0:
                    eng.wait_ge(s, count * unit)
            else:
                eng.wait_ge(s, batch * (per * unit) + k * unit)

        def live(batch):
            return not isinstance(batch, int) or 0 <= batch < NB

        def front_in_step(n):
            return live(n + 2) and not (isinstance(n, int) and n == -1)

        def y_bank(batch, r):
            return (peak_ps + st_ps)[r] if isinstance(batch, int) and batch >= NB - 2 else y_ps

        def rows(ap, tile):
            return ap[:, bass.ds(tile, TILES), :]

        def tile_of(eng, batch):
            return batch * TILES if isinstance(batch, int) else eng.snap(batch * TILES)

        def steps(eng, step):
            for n in range(-2, 2):
                step(n, n % 2, n // 2)
            with eng.Fori(1, NB // 2 - 1) as two:
                step(two * 2, 0, two)
                step(two * 2 + 1, 1, two)
            for n in range(NB - 2, NB + 2):
                step(n, n % 2, n // 2)

        block = es.enter_context(nc.Block())

        @block.sync
        def _(sp):
            x_rows = x.rearrange("b (t p) d -> p (b t) d", p=P)
            c_rows = ctx_in.rearrange("b (t p) d -> p (b t) d", p=P)


            def load_first():
                sp.dma_start(xin[0][:], rows(x_rows, 0)).then_inc(x_in[0], DMA)
                sp.dma_start(cin[0][:], rows(c_rows, 0)).then_inc(c_in[0], DMA)
                for col, vector in ((bq_col, bq), (bk_col, bk)):
                    sp.dma_start(col[:], vector.rearrange("(p r d) -> r d p", r=2, d=HD),
                                 allow_slow_non_contiguous=True).then_inc(bias_in, DMA)
                sp.dma_start(xin[1][:], rows(x_rows, TILES)).then_inc(x_in[1], DMA)
                sp.dma_start(cin[1][:], rows(c_rows, TILES)).then_inc(c_in[1], DMA)
                sp.dma_start(w_raw[:, 2], Wv).then_inc(wvo_in, DMA)
                sp.dma_start(w_raw[:, 3], Wo).then_inc(wvo_in, DMA)
                sp.dma_start(we_raw[:], W.rearrange("e f h -> f e h")).then_inc(we_in, DMA)
                sp.dma_start(gates[:, 0:1], g_xattn.unsqueeze(0).broadcast_to([P, 1])).then_inc(small_in, DMA)
                sp.dma_start(gates[:, 1:2], g_ffn.unsqueeze(0).broadcast_to([P, 1])).then_inc(small_in, DMA)
                sp.dma_start(bv_row[:], bv.unsqueeze(0).broadcast_to([P, D])).then_inc(small_in, DMA)
                sp.dma_start(bo_row[:], bo.unsqueeze(0).broadcast_to([P, D])).then_inc(small_in, DMA)
                sp.dma_start(wg_sb[:], wg).then_inc(small_in, DMA)
                sp.dma_start(be_sb[:], b_exp).then_inc(small_in, DMA)

            def load_stack(batch, par, half):
                wait(sp, st_mm, batch - 2, UNITS // 2 * (half + 1), UNITS)
                wait(sp, split_out, batch, 6, 6, DMA)
                if isinstance(batch, int) and batch < 2:
                    sp.wait_ge(cleared, 4)
                pairs = slice(half * HALF, (half + 1) * HALF)
                for r in range(2):
                    for dst, scr in ((kst[par][r * HROWS:(r + 1) * HROWS, pairs, :], k_scr[par]),
                                     (qz[par][r * HROWS:(r + 1) * HROWS, half, r, :, :], q_scr[par])):
                        src = scr.rearrange("s (r d p) q -> r s d p q", r=2, d=HD)[r, :, :, pairs, :]
                        sp.dma_start(dst, src.rearrange("s d p q -> s d (p q)")).then_inc(stack_in[half], DMA)

            def load_max(batch, par, half):
                wait(sp, mT_ready, batch, half + 1, 2)
                sp.dma_start(qz[par][QROWS:KROWS, half].rearrange("a r p q -> a (r p) q"),
                             mT[half][:]).then_inc(max_in[half], DMA)

            def step(n, cur, two):
                nxt = 1 - cur
                front_tile, attend_tile = tile_of(sp, n + 2), tile_of(sp, n)
                if isinstance(n, int) and n == -2:
                    load_first()
                elif live(n + 2) and not (isinstance(n, int) and n == -1):
                    wait(sp, xn_ready, n)
                    sp.dma_start(xin[cur][:], rows(x_rows, front_tile)).then_inc(x_in[cur], DMA)
                    wait(sp, frontT_mm, n)
                    sp.dma_start(cin[cur][:], rows(c_rows, front_tile)).then_inc(c_in[cur], DMA)
                if live(n + 1):
                    load_stack(n + 1, nxt, 1)
                if live(n):
                    wait(sp, x2_ready, n - 2)
                    wait(sp, xres_ready, n - 1)
                    sp.dma_start(xres[cur][:], rows(x_rows, attend_tile)).then_inc(xr_in, DMA)
                    load_max(n, cur, 1)
                if live(n + 2):
                    for part, ready, q_slots, k_slots in (
                            (0, part1_ready, slice(0, 3), slice(1, 6, 2)),
                            (1, part2_ready, slice(3, 5), slice(2, 5, 2)),
                            (2, part3_ready, slice(5, 6), slice(0, 1))):
                        wait(sp, ready, n + 2)
                        for t, scr, slots in ((0, q_scr[cur], q_slots), (1, k_scr[cur], k_slots)):
                            dst = scr[slots].rearrange("s z q -> z s q")
                            src = parts[:, part, t, :].unsqueeze(1).broadcast_to(list(dst.shape))
                            sp.dma_start(dst, src).then_inc(split_out, DMA)
                if live(n + 1):
                    load_max(n + 1, nxt, 0)
                if live(n + 2):
                    load_stack(n + 2, cur, 0)

            steps(sp, step)

        @block.gpsimd
        def _(pool):
            o_rows = out.rearrange("b (t p) d -> p (b t) d", p=P)
            nc.gpsimd.memset(ident[:], 0.0).then_inc(drawn, 1)
            pool.wait_ge(drawn, 1)
            nc.gpsimd.affine_select(out=ident[:], in_=ident[:], compare_op=ALU.not_equal, fill=1.0, base=0,
                                    pattern=[[-1, P]], channel_multiplier=1).then_inc(ident_ready, 1)
            nc.gpsimd.memset(minus_half[:], -0.5).then_inc(ident_ready, 1)
            for i in range(2):
                nc.gpsimd.memset(kst[i][:], 1.0).then_inc(cleared, 1)
            nc.gpsimd.memset(ones[:], 1.0).then_inc(drawn, 1)
            pool.wait_ge(ident_ready, 2)
            nc.gpsimd.tensor_copy(identb[:], ident[:]).then_inc(const_ready, 1)
            pool.wait_ge(drawn, 2)
            nc.gpsimd.affine_select(out=before[:], in_=ones[:], compare_op=ALU.is_gt, fill=0.0, base=0,
                                    pattern=[[1, P]], channel_multiplier=-1).then_inc(const_ready, 1)
            for e in range(EXPERTS):
                nc.gpsimd.memset(rank[:, :, e:e + 1], float(EXPERTS - e)).then_inc(const_ready, 1)

            def split(batch):
                wait(pool, part1_ready, batch)
                wait(pool, part2_ready, batch - 1)
                nc.gpsimd.tensor_tensor(rest[:], qk[:], parts[:, 0], ALU.subtract).then_inc(rest_ready, 1)
                wait(pool, part2_ready, batch)
                wait(pool, split_out, batch - 1, 6, 6, DMA)
                nc.gpsimd.tensor_tensor(parts[:, 2], rest[:], parts[:, 1], ALU.subtract).then_inc(part3_ready, 1)

            def fold(batch, r):
                t, half = r // 2, r % 2
                wait(pool, scaled_ready, batch, r + 1, 4)
                nc.gpsimd.tensor_tensor(fold2[:], scaled[t][:, 4 * half:4 * half + 2],
                                        scaled[t][:, 4 * half + 2:4 * half + 4], ALU.add).then_inc(folded, 1)
                wait(pool, folded, batch, 2 * r + 1, 8)
                nc.gpsimd.tensor_tensor(fold1[:], fold2[:, 0], fold2[:, 1], ALU.add).then_inc(folded, 1)
                wait(pool, folded, batch, 2 * r + 2, 8)
                if half == 0:
                    wait(pool, base_ready, batch)
                    nc.gpsimd.tensor_tensor(first_sum[:, t], fold1[:], base[:, t], ALU.add).then_inc(first_half, 1)
                else:
                    wait(pool, first_half, batch, t + 1, TILES)
                    nc.gpsimd.tensor_tensor(rows(res[:], batch * TILES)[:, t], fold1[:], first_sum[:, t],
                                            ALU.add).then_inc(res_ready, 1)

            def step(n, cur, two):
                nxt = 1 - cur
                expert_tile = tile_of(pool, n - 2)
                if live(n + 2):
                    wait(pool, var1_ready, n + 2)
                    nc.gpsimd.tensor_tensor(rstd1[:], var1[:], minus_half[:], ALU.pow).then_inc(rstd1_ready, 1)
                if live(n - 1):
                    wait(pool, xr_in, n - 1, 1, 1, DMA)
                    if isinstance(n, int):
                        pool.wait_ge(gbo_ready, 1)
                    nc.gpsimd.tensor_tensor(xres[nxt][:], xres[nxt][:],
                                            gbo_row[:].unsqueeze(1).broadcast_to([P, TILES, D]),
                                            ALU.add).then_inc(xres_ready, 1)
                if live(n + 2):
                    split(n + 2)
                if live(n - 1):
                    wait(pool, var2_ready, n - 1)
                    nc.gpsimd.tensor_tensor(rstd2[:], var2[:], minus_half[:], ALU.pow).then_inc(rstd2_ready, 1)
                if live(n - 2):
                    for r in range(2 if isinstance(n, int) and n == NB + 1 else 4):
                        fold(n - 2, r)
                    wait(pool, res_ready, n - 2, 2, 2)
                    pool.dma_start(rows(o_rows, expert_tile), rows(res[:], expert_tile)).then_inc(stored, DMA)

            steps(pool, step)
            pool.wait_ge(stored, NB * DMA)

        @block.scalar
        def _(act):
            act.dma_start(w_raw[:, 0], Wq).then_inc(wqk_in, DMA)
            act.dma_start(w_raw[:, 1], Wk).then_inc(wqk_in, DMA)
            act.wait_ge(ident_ready, 1)
            nc.scalar.activation(warm[:], ident[:, 0:1], ACT.Exp)
            act.wait_ge(wT_mm, 2)
            nc.scalar.copy(wqT[:], front_ps[:, 0:D].rearrange("z (p r d) -> z r d p", r=2, d=HD)).then_inc(wT_ready, 1)
            nc.scalar.copy(wkT[:], front_ps[:, D:2 * D].rearrange("z (p r d) -> z r d p", r=2, d=HD)).then_inc(wT_ready, 1)
            act.wait_ge(bias_in, 2 * DMA)

            def late_setup():
                act.wait_ge(wT_mm, 4)
                nc.scalar.copy(wvT[:], post_ps[:, 0:D]).then_inc(wT_ready, 1)
                nc.scalar.copy(woT[:], post_ps[:, D:2 * D]).then_inc(wT_ready, 1)
                for half in range(2):
                    act.wait_ge(weT_mm, half + 1)
                    nc.scalar.copy(weT[:, 4 * half:4 * half + 4, :], st_ps[half][:]).then_inc(weT_ready, 1)
                act.wait_ge(small_in, 6 * DMA)
                nc.scalar.activation(tg[:], gates[:], ACT.Tanh).then_inc(tg_ready, 1)

            def copy_max(batch, half):
                wait(act, mT_mm, batch, half + 1, 2)
                wait(act, max_in[half], batch - 1, 1, 1, DMA)
                nc.scalar.copy(mT[half][:], front_b[0:4 * HALF, 0:SEQ]).then_inc(mT_ready, 1)

            def copy_front(batch, par):
                wait(act, frontT_mm, batch)
                nc.scalar.copy(frontT[par][:], front_ps[:]).then_inc(frontT_ready, 1)

            def copy_qk(batch):
                wait(act, qk_mm, batch)
                wait(act, rest_ready, batch - 1)
                for t, bias in ((0, bq_col), (1, bk_col)):
                    last = nc.scalar.activation(qk[:, t], front_ps[:, t * SEQ:(t + 1) * SEQ], ACT.Identity,
                                                bias=bias[:, 0:1])
                last.then_inc(qk_ready, 1)
                first_part(batch)

            def first_part(batch):
                wait(act, qk_ready, batch)
                wait(act, split_out, batch - 1, 6, 6, DMA)
                nc.scalar.copy(parts[:, 0], qk[:]).then_inc(part1_ready, 1)

            def scale(batch, r):
                t, first = r // 2, 4 * (r % 2)
                wait(act, y_mm, batch, r + 1, 4)
                if isinstance(batch, int):
                    wait(act, folded, batch - 1, 2 * r + 1, 8)
                for i in range(4):
                    last = nc.scalar.activation(scaled[t][:, first + i], y_bank(batch, r)[:, i * D:(i + 1) * D], ACT.Copy,
                                                scale=share[:, t, first + i:first + i + 1])
                last.then_inc(scaled_ready, 1)

            def step(n, cur, two):
                nxt = 1 - cur
                if isinstance(n, int) and n == -1:
                    copy_front(1, 1)
                    copy_qk(1)
                for s in range(UNITS):
                    if live(n):
                        wait(act, st_mm, n, s + 1, UNITS)
                        wait(act, pv_mm, n - 1, s // 4 + 1, 4)
                        nc.scalar.activation(probs[:, s], st_ps[s % 2][:], ACT.Exp,
                                             scale=SCALE).then_inc(exp_ready, 1)
                    if s == 2 and live(n):
                        copy_max(n, 1)
                    if s == 1 and live(n - 1):
                        wait(act, pv_mm, n - 1, 4, 4)
                        wait(act, oT_mm, n - 2)
                        nc.scalar.copy(o_sb[:], o_ps[:]).then_inc(o_ready, 1)
                    if s == 3 and live(n - 2):
                        wait(act, shareT_mm, n - 2)
                        nc.scalar.copy(shareT[:], y_ps[0:EXPERTS, 0:SEQ]).then_inc(shareT_ready, 1)
                    if s == 4 and front_in_step(n):
                        copy_front(n + 2, cur)
                    if s == 6 and live(n - 1):
                        wait(act, attnT_mm, n - 1)
                        nc.scalar.copy(attnT[:], post_ps[:, 0:SEQ]).then_inc(attnT_ready, 1)
                    if s == 6 and front_in_step(n):
                        copy_qk(n + 2)
                    if s in EXPERT_AT and live(n - 2):
                        r = EXPERT_AT.index(s)
                        if not (isinstance(n, int) and n == NB + 1 and r >= 2):
                            scale(n - 2, r)
                    if s == 9 and live(n + 1):
                        copy_max(n + 1, 0)
                    if s == 11 and live(n - 1):
                        wait(act, x2T_mm, n - 1)
                        nc.scalar.copy(x2T[nxt][:], post_ps[:, 0:SEQ]).then_inc(x2T_ready, 1)
                    if s == 15 and live(n - 1):
                        wait(act, lsub_ready, n - 1)
                        nc.scalar.activation(lexp[:], lsub[:], ACT.Exp).then_inc(lexp_ready, 1)
                if isinstance(n, int) and n == -2:
                    late_setup()

            steps(act, step)

        @block.vector
        def _(dve):
            def peak(batch, s):
                half, p, r = s // 8, (s % 8) // 2, s % 2
                wait(dve, peak_mm, batch, s + 1, UNITS)
                nc.vector.tensor_reduce(negmax[:, half, :, r, p], peak_ps[s % 2][:].rearrange("z (t k) -> z t k", t=TILES),
                                        axis=AX.X, op=ALU.max, negate=True).then_inc(peak_read, 1)

            def split_max(batch, half):
                src = negmax[:, half].rearrange("z t r p -> z t (r p)")
                wait(dve, peak_read, batch, 8 * (half + 1), UNITS)
                nc.vector.tensor_copy(mneg[:, half, :, 0, :], src).then_inc(hi_ready, 1)
                wait(dve, hi_ready, batch, half + 1, 2)
                nc.vector.tensor_tensor(mneg[:, half, :, 1, :], src, mneg[:, half, :, 0, :],
                                        ALU.subtract).then_inc(mneg_ready, 1)

            def statistics(src, stat, stat_done):
                for t in range(TILES):
                    last = nc.vector.bn_stats(stat[:, t], src[:, t])
                last.then_inc(stat_done, 1)

            def variance(batch, stat, mv, var, mv_done, var_ready):
                for t in range(TILES):
                    last = nc.vector.bn_aggr(mv[:, t], stat[:, t])
                last.then_inc(mv_done, 1)
                wait(dve, mv_done, batch)
                nc.vector.tensor_scalar(var[:], mv[:, :, 1], EPS, None, ALU.add).then_inc(var_ready, 1)

            def norm(dst, src, mv, rstd, ready):
                for t in range(TILES):
                    last = nc.vector.tensor_scalar(dst[:, t], src[:, t], mv[:, t, 0:1], rstd[:, t:t + 1],
                                                   ALU.subtract, ALU.mult)
                last.then_inc(ready, 1)

            def front_norm(batch, par):
                wait(dve, rstd1_ready, batch)
                wait(dve, frontT_mm, batch - 1)
                norm(xn, xin[par], mv1, rstd1, xn_ready)

            def second_part(batch):
                wait(dve, rest_ready, batch)
                nc.vector.tensor_copy(parts[:, 1], rest[:]).then_inc(part2_ready, 1)

            def place_v(batch, par):
                wait(dve, v_mm, batch)
                wait(dve, pv_mm, batch - 2, 4, 4)
                if isinstance(batch, int) and batch == 0:
                    dve.wait_ge(small_in, 6 * DMA)
                for t in range(TILES):
                    dst = vaug[par][:, t].rearrange("z (p r) c -> z p (r c)", r=2)
                    for r in range(2):
                        last = nc.vector.tensor_tensor(
                            dst[:, :, r * (32 + HD):r * (32 + HD) + HD],
                            front_ps[:, t * D:(t + 1) * D].rearrange("z (p r d) -> z r p d", r=2, d=HD)[:, r],
                            bv_row[:].rearrange("z (p r d) -> z r p d", r=2, d=HD)[:, r], ALU.add)
                last.then_inc(v_ready, 1)

            def normalise(batch):
                wait(dve, oT_mm, batch)
                oT = post_ps[:].rearrange("z (g c) -> z g c", c=32)
                nc.vector.reciprocal(rsum[:], oT[:, :, 2 * HD:2 * HD + 2]).then_inc(rsum_ready, 1)
                wait(dve, rsum_ready, batch)
                wait(dve, attnT_mm, batch - 1)
                nc.vector.tensor_tensor(
                    attn[:].rearrange("z t (g r d) -> z (t g) r d", r=2, d=HD),
                    oT[:, :, 0:2 * HD].rearrange("z g (r d) -> z g r d", r=2),
                    rsum[:].unsqueeze(3).broadcast_to([P, TILES * PAIRS, 2, HD]), ALU.mult).then_inc(attn_ready, 1)

            def residual(batch, par):
                wait(dve, proj_mm, batch)
                wait(dve, xres_ready, batch)
                nc.vector.scalar_tensor_tensor(x2[par][:].rearrange("z t d -> z (t d)"), post_ps[:, 0:SEQ], tg[:, 0:1],
                                               xres[par][:].rearrange("z t d -> z (t d)"),
                                               ALU.mult, ALU.add).then_inc(x2_ready, 1)
                wait(dve, x2_ready, batch)
                statistics(x2[par], stat2, stat2_done)

            def choose(batch):
                wait(dve, logit_mm, batch)
                logits = post_ps[:, 0:TILES * EXPERTS].rearrange("z (t e) -> z t e", t=TILES)
                nc.vector.tensor_reduce(lmax[:], logits, axis=AX.X, op=ALU.max).then_inc(lmax_done, 1)
                wait(dve, lmax_done, batch)
                nc.vector.tensor_tensor(lsub[:], logits, lmax[:].unsqueeze(2).broadcast_to([P, TILES, EXPERTS]),
                                        ALU.subtract).then_inc(lsub_ready, 1)
                wait(dve, lsub_ready, batch)
                nc.vector.scalar_tensor_tensor(score[:], lsub[:], 0.0, rank[:], ALU.is_ge, ALU.mult).then_inc(score_done, 1)
                wait(dve, score_done, batch)
                nc.vector.tensor_reduce(smax[:], score[:], axis=AX.X, op=ALU.max).then_inc(smax_done, 1)
                wait(dve, smax_done, batch)
                nc.vector.tensor_tensor(chosen[:], score[:], smax[:].unsqueeze(2).broadcast_to([P, TILES, EXPERTS]),
                                        ALU.is_equal).then_inc(chosen_ready, 1)

            def weigh(batch):
                wait(dve, lexp_ready, batch)
                nc.vector.tensor_reduce(lsum[:], lexp[:], axis=AX.X, op=ALU.add).then_inc(lsum_done, 1)
                wait(dve, lsum_done, batch)
                nc.vector.reciprocal(lrec[:], lsum[:]).then_inc(lrec_done, 1)
                wait(dve, lrec_done, batch)
                nc.vector.tensor_scalar(gate[:], lrec[:], tg[:, 1:2], None, ALU.mult).then_inc(gate_ready, 1)

            def keep(batch, par):
                wait(dve, loc_mm, batch)
                loc = post_ps[:, 0:TILES * EXPERTS].rearrange("z (t e) -> z t e", t=TILES)
                nc.vector.scalar_tensor_tensor(kept[:], loc, float(CAPACITY), chosen[:],
                                               ALU.is_lt, ALU.mult).then_inc(kept_ready, 1)
                nc.vector.tensor_tensor(counts[:], counts[:], chosen[:, 0], ALU.add).then_inc(counts_done, 1)
                wait(dve, kept_ready, batch)
                wait(dve, gate_ready, batch)
                nc.vector.tensor_tensor(share[:], kept[:], gate[:].unsqueeze(2).broadcast_to([P, TILES, EXPERTS]),
                                        ALU.mult).then_inc(share_ready, 1)
                wait(dve, counts_done, batch, 1, TILES)
                nc.vector.tensor_tensor(counts[:], counts[:], chosen[:, 1], ALU.add).then_inc(counts_done, 1)

            def take_base(batch, par):
                wait(dve, bias_mm, batch)
                if isinstance(batch, int):
                    wait(dve, res_ready, batch - 1, 2, 2)
                nc.vector.tensor_tensor(base[:].rearrange("z t d -> z (t d)"), y_ps[:, 0:SEQ],
                                        x2[par][:].rearrange("z t d -> z (t d)"), ALU.add).then_inc(base_ready, 1)

            def clear():
                for i in range(2):
                    nc.vector.memset(qz[i][:].rearrange("z h r p q -> z (h r p q)").bitcast(mybir.dt.uint32), 0).then_inc(cleared, 1)
                    nc.vector.memset(vaug[i][:], 0.0).then_inc(framed, 1)
                nc.vector.memset(counts[:], 0.0)
                dve.wait_ge(framed, 2)
                for i in range(2):
                    frame = vaug[i][:].rearrange("z t (p r) c -> z t p (r c)", r=2)
                    for r in range(2):
                        column = r * 32 + 2 * HD + r
                        nc.vector.memset(frame[:, :, :, column:column + 1], 1.0)

            def first_norm():
                dve.wait_ge(x_in[1], DMA)
                statistics(xin[1], stat1, stat1_done)
                wait(dve, stat1_done, 1)
                variance(1, stat1, mv1, var1, mv1_done, var1_ready)
                front_norm(1, 1)
                second_part(1)

            def last_tile():
                batch, t = NB - 1, 1
                for r in (2, 3):
                    first = 4 * (r % 2)
                    wait(dve, y_mm, batch, r + 1, 4)
                    wait(dve, folded, batch - 1, 2 * r + 1, 8)
                    nc.vector.tensor_tensor(scaled[t][:, first:first + 4],
                                            y_bank(batch, r)[:].rearrange("z (e d) -> z e d", e=4),
                                            share[:, t, first:first + 4].unsqueeze(2).broadcast_to([P, 4, D]),
                                            ALU.mult).then_inc(tail, 1)
                steps_of = ((tail4, scaled[t][:, 0:4], scaled[t][:, 4:8]), (tail2, tail4[:, 0:2], tail4[:, 2:4]),
                            (tail1, tail2[:, 0:1], tail2[:, 1:2]))
                for i, (dst, a, b) in enumerate(steps_of):
                    dve.wait_ge(tail, 2 + i)
                    nc.vector.tensor_tensor(dst[:], a, b, ALU.add).then_inc(tail, 1)
                dve.wait_ge(tail, 5)
                wait(dve, base_ready, batch)
                nc.vector.tensor_tensor(rows(res[:], batch * TILES)[:, t], tail1[:, 0], base[:, t],
                                        ALU.add).then_inc(res_ready, 1)

            def gated_bias():
                dve.wait_ge(small_in, 6 * DMA)
                dve.wait_ge(tg_ready, 1)
                nc.vector.tensor_scalar(gbo_row[:], bo_row[:], tg[:, 0:1], None, ALU.mult).then_inc(gbo_ready, 1)

            def step(n, cur, two):
                nxt = 1 - cur
                if isinstance(n, int) and n == -1:
                    first_norm()
                if live(n):
                    split_max(n, 1)
                for s in range(UNITS):
                    if s == 9 and live(n - 1):
                        wait(dve, stat2_done, n - 1)
                    if s == 1 and front_in_step(n):
                        wait(dve, stat1_done, n + 2)
                    if live(n + 1):
                        peak(n + 1, s)
                    if s == 0 and live(n - 2):
                        weigh(n - 2)
                    if s == 0 and front_in_step(n):
                        wait(dve, x_in[cur], two + 1, 1, 1, DMA)
                        statistics(xin[cur], stat1, stat1_done)
                    if s == 1 and live(n - 2):
                        keep(n - 2, cur)
                    if s == 1 and front_in_step(n):
                        variance(n + 2, stat1, mv1, var1, mv1_done, var1_ready)
                    if s == 2 and front_in_step(n):
                        front_norm(n + 2, cur)
                        if isinstance(n, int) and n == -2:
                            clear()
                    if s == 3 and live(n - 1):
                        normalise(n - 1)
                    if s == 5 and live(n - 2):
                        take_base(n - 2, cur)
                    if s == 7 and live(n + 1):
                        split_max(n + 1, 0)
                    if s == 8 and live(n - 1):
                        residual(n - 1, nxt)
                    if s == 8 and front_in_step(n):
                        second_part(n + 2)
                    if s == 9 and live(n - 1):
                        variance(n - 1, stat2, mv2, var2, mv2_done, var2_ready)
                    if s == 10 and live(n - 1):
                        wait(dve, rstd2_ready, n - 1)
                        wait(dve, x2T_mm, n - 2)
                        norm(x2n, x2[nxt], mv2, rstd2, x2n_ready)
                    if s == 12 and live(n + 1):
                        place_v(n + 1, nxt)
                    if s == 13 and live(n - 1):
                        choose(n - 1)
                if isinstance(n, int) and n == NB + 1:
                    last_tile()
                if isinstance(n, int) and n == -2:
                    gated_bias()

            steps(dve, step)

        @block.tensor
        def _(pe):
            def turn_weights(pairs, ready):
                for dst, src in pairs:
                    last = nc.tensor.transpose(dst, src, ident[:])
                last.then_inc(ready, 1)

            pe.wait_ge(ident_ready, 1)
            pe.wait_ge(wqk_in, 2 * DMA)
            turn_weights([(front_ps[:, 0:D], w_raw[:, 0])], wT_mm)
            turn_weights([(front_ps[:, D:2 * D], w_raw[:, 1])], wT_mm)
            pe.wait_ge(wT_ready, 2)

            def late_setup():
                pe.wait_ge(wvo_in, 2 * DMA)
                turn_weights([(post_ps[:, 0:D], w_raw[:, 2])], wT_mm)
                turn_weights([(post_ps[:, D:2 * D], w_raw[:, 3])], wT_mm)
                pe.wait_ge(we_in, DMA)
                for half in range(2):
                    turn_weights([(st_ps[half][:, i * D:(i + 1) * D], we_raw[:, 4 * half + i]) for i in range(4)], weT_mm)

            def peak(batch, par, s):
                half, p, r = s // 8, s // 2, s % 2
                if s % 8 == 0:
                    wait(pe, stack_in[half], batch, 4, 4, DMA)
                wait(pe, peak_read, batch, s - 1, UNITS)
                for t in range(TILES):
                    last = nc.tensor.matmul(peak_ps[s % 2][:, t * SEQ:(t + 1) * SEQ],
                                            qz[par][0:QROWS, half, r, p % HALF, t * P:(t + 1) * P], kst[par][0:QROWS, p, :],
                                            start=True, stop=True)
                last.then_inc(peak_mm, 1)

            def scores(batch, par, s):
                half, t, g = s // 8, (s % 8) // 4, s % 4
                p = half * HALF + g
                if s % 8 == 0:
                    wait(pe, max_in[half], batch, 1, 1, DMA)
                wait(pe, exp_ready, batch, s - 1, UNITS)
                nc.tensor.matmul(st_ps[s % 2][:], kst[par][0:KROWS, p, t * P:(t + 1) * P], qz[par][0:KROWS, half, :, g, :],
                                 start=True, stop=True).then_inc(st_mm, 1)

            def values(batch, par, quarter):
                half, t = quarter // 2, quarter % 2
                wait(pe, exp_ready, batch, 4 * quarter + 4, UNITS)
                if quarter == 0:
                    wait(pe, v_ready, batch)
                    wait(pe, o_ready, batch - 1)
                for r in range(2):
                    for g in range(4):
                        last = nc.tensor.matmul(o_ps[32 * g:32 * g + 32, half * SEQ:(half + 1) * SEQ],
                                                vaug[par][:, t, 2 * (half * HALF + g) + r, :],
                                                probs[:, 4 * quarter + g, r, :],
                                                start=(t == 0 and r == 0), stop=(t == 1 and r == 1))
                last.then_inc(pv_mm, 1)

            def turn_max(batch, half):
                if half == 0:
                    wait(pe, qk_ready, batch + 1)
                else:
                    wait(pe, v_ready, batch)
                wait(pe, mneg_ready, batch, half + 1, 2)
                for t in range(TILES):
                    last = nc.tensor.transpose(front_b[0:4 * HALF, t * P:(t + 1) * P],
                                               mneg[:, half, t].rearrange("z a h -> z (a h)"), identb[:])
                last.then_inc(mT_mm, 1)

            def turn_front(batch, par, two):
                if isinstance(batch, int) and batch == 1:
                    wait(pe, qk_ready, 0)
                wait(pe, mT_ready, batch - 2, 2, 2)
                wait(pe, xn_ready, batch)
                wait(pe, c_in[par], two, 1, 1, DMA)
                for i, src in ((0, xn), (1, cin[par])):
                    for t in range(TILES):
                        last = nc.tensor.transpose(front_ps[:, i * SEQ + t * P:i * SEQ + (t + 1) * P], src[:, t], ident[:])
                last.then_inc(frontT_mm, 1)

            def project_qk(batch, par):
                wait(pe, frontT_ready, batch)
                for i, w in ((0, wqT), (1, wkT)):
                    last = nc.tensor.matmul(front_ps[:, i * SEQ:(i + 1) * SEQ], w[:].rearrange("z r d p -> z (r d p)"),
                                            frontT[par][:, i], start=True, stop=True)
                last.then_inc(qk_mm, 1)

            def project_v(batch, par):
                if isinstance(batch, int) and batch == 0:
                    pe.wait_ge(wT_ready, 4)
                wait(pe, mT_ready, batch, 1, 2)
                for t in range(TILES):
                    last = nc.tensor.matmul(front_ps[:, t * D:(t + 1) * D], frontT[par][:, 1, t * P:(t + 1) * P], wvT[:],
                                            start=True, stop=True)
                last.then_inc(v_mm, 1)

            def turn_o(batch):
                wait(pe, o_ready, batch)
                wait(pe, kept_ready, batch - 1)
                for t in range(TILES):
                    for half in range(2):
                        last = nc.tensor.transpose(post_ps[:, (t * 2 + half) * P:(t * 2 + half + 1) * P],
                                                   o_sb[:, half, t * P:(t + 1) * P], ident[:])
                last.then_inc(oT_mm, 1)

            def turn_attn(batch):
                wait(pe, attn_ready, batch)
                for t in range(TILES):
                    last = nc.tensor.transpose(post_ps[:, t * P:(t + 1) * P], attn[:, t], ident[:])
                last.then_inc(attnT_mm, 1)

            def project_o(batch):
                wait(pe, attnT_ready, batch)
                for t in range(TILES):
                    last = nc.tensor.matmul(post_ps[:, t * D:(t + 1) * D], attnT[:, t * P:(t + 1) * P], woT[:],
                                            start=True, stop=True)
                last.then_inc(proj_mm, 1)

            def turn_x2(batch):
                wait(pe, x2n_ready, batch)
                for t in range(TILES):
                    last = nc.tensor.transpose(post_ps[:, t * P:(t + 1) * P], x2n[:, t], ident[:])
                last.then_inc(x2T_mm, 1)

            def route(batch, par):
                wait(pe, x2T_ready, batch)
                for t in range(TILES):
                    last = nc.tensor.matmul(post_ps[:, t * EXPERTS:(t + 1) * EXPERTS], x2T[par][:, t * P:(t + 1) * P],
                                            wg_sb[:], start=True, stop=True)
                last.then_inc(logit_mm, 1)

            def locate(batch):
                wait(pe, chosen_ready, batch)
                for t in range(TILES):
                    dst = post_ps[:, t * EXPERTS:(t + 1) * EXPERTS]
                    nc.tensor.matmul(dst, before[:], chosen[:, t], start=True, stop=False)
                    if t == 1:
                        nc.tensor.matmul(dst, ones[:], chosen[:, 0], start=False, stop=False)
                    last = nc.tensor.matmul(dst, ones[:], counts[:], start=False, stop=True)
                last.then_inc(loc_mm, 1)

            def turn_share(batch):
                wait(pe, share_ready, batch)
                for t in range(TILES):
                    last = nc.tensor.transpose(y_ps[0:EXPERTS, t * P:(t + 1) * P], share[:, t], ident[:])
                last.then_inc(shareT_mm, 1)

            def expert_bias(batch):
                wait(pe, shareT_ready, batch)
                for t in range(TILES):
                    last = nc.tensor.matmul(y_ps[:, t * D:(t + 1) * D], shareT[:, t * P:(t + 1) * P], be_sb[:],
                                            start=True, stop=True)
                last.then_inc(bias_mm, 1)

            def expert(batch, par, r):
                t, first = r // 2, 4 * (r % 2)
                if isinstance(batch, int) and batch == NB - 1:
                    wait(pe, x2T_ready, batch)
                    wait(pe, scaled_ready, batch - 1, r + 1, 4)
                elif isinstance(batch, int) and batch == NB - 2:
                    wait(pe, peak_read, NB - 1, UNITS, UNITS)
                    wait(pe, exp_ready, NB - 1, UNITS, UNITS)
                elif r == 0:
                    wait(pe, base_ready, batch)
                else:
                    wait(pe, scaled_ready, batch, r, 4)
                nc.tensor.matmul(y_bank(batch, r)[:], x2T[par][:, t * P:(t + 1) * P],
                                 weT[:, first:first + 4].rearrange("z e d -> z (e d)"), start=True, stop=True).then_inc(y_mm, 1)

            def step(n, cur, two):
                nxt = 1 - cur
                if isinstance(n, int) and n == 0:
                    pe.wait_ge(weT_ready, 2)
                if isinstance(n, int) and n == -1:
                    turn_front(1, 1, 0)
                    project_qk(1, 1)
                for s in range(UNITS):
                    if live(n + 1):
                        peak(n + 1, nxt, s)
                    if live(n):
                        scores(n, cur, s)
                    if s == 0 and live(n - 2):
                        locate(n - 2)
                    if s == 2 and live(n):
                        turn_max(n, 1)
                    if s == 1 and live(n - 1):
                        values(n - 1, nxt, 3)
                    if s in VALUES_AT and live(n):
                        values(n, cur, VALUES_AT.index(s))
                    if s == 3 and live(n - 2):
                        turn_share(n - 2)
                    if s == 3 and live(n - 1):
                        turn_o(n - 1)
                    if s == 4 and front_in_step(n):
                        turn_front(n + 2, cur, two + 1)
                    if s == 5 and live(n - 2):
                        expert_bias(n - 2)
                    if s == 6 and live(n - 1):
                        turn_attn(n - 1)
                    if s == 6 and front_in_step(n):
                        project_qk(n + 2, cur)
                    if s == 8 and live(n - 1):
                        project_o(n - 1)
                    if s in EXPERT_AT and live(n - 2) and not (isinstance(n, int) and n == NB + 1):
                        expert(n - 2, cur, EXPERT_AT.index(s))
                    if s == 9 and live(n + 1):
                        if isinstance(n, int) and n == -1:
                            pe.wait_ge(const_ready, 10)
                            pe.wait_ge(small_in, 6 * DMA)
                        turn_max(n + 1, 0)
                    if s == 11 and live(n - 1):
                        turn_x2(n - 1)
                    if s == 12 and live(n + 1):
                        project_v(n + 1, nxt)
                    if s == 13 and live(n - 1):
                        route(n - 1, nxt)
                if isinstance(n, int) and n == NB:
                    for r in range(4):
                        expert(n - 1, nxt, r)
                if isinstance(n, int) and n == -2:
                    late_setup()

            steps(pe, step)


_INS = ['x', 'ctx_1024', 'g_xattn', 'g_ffn', 'L0_xattn_Wq', 'L0_xattn_bq', 'L0_xattn_Wk', 'L0_xattn_bk',
        'L0_xattn_Wv', 'L0_xattn_bv', 'L0_xattn_Wo', 'L0_xattn_bo', 'L0_ffn_wg', 'L0_ffn_W', 'L0_ffn_b']


def kernel(**inputs):
    import numpy as _np
    import concourse.bacc as _bacc
    from concourse.bass_utils import run_bass_kernel_spmd as _run

    nc = _bacc.Bacc("TRN2", target_bir_lowering=False, num_devices=1)
    arrays, args = {}, []
    for name in _INS:
        a = _np.ascontiguousarray(inputs[name])
        arrays[f"in_{name}"] = a
        args.append(nc.dram_tensor(f"in_{name}", a.shape, mybir.dt.from_np(a.dtype), kind="ExternalInput").ap())
    o = nc.dram_tensor("out_0", (NB, SEQ, D), F32, kind="ExternalOutput").ap()
    build(nc, *args, o)
    r = _run(nc, [arrays], core_ids=[0])
    return r.results[0]["out_0"]
```

```python
from contextlib import ExitStack

import concourse.bass as bass
from concourse import mybir

ALU = mybir.AluOpType
ACT = mybir.ActivationFunctionType
AX = mybir.AxisListType
F32 = mybir.dt.float32
BF16 = mybir.dt.bfloat16

P = 128
NB = 8
SEQ = 256
D = 128
H = 16
HD = D // H
TILES = SEQ // P
PAIRS = H // 2
HALF = PAIRS // 2
EXPERTS = 8
CAPACITY = NB * SEQ // EXPERTS
SLOTS = 6
HROWS = SLOTS * HD
QROWS = 2 * HROWS
KROWS = QROWS + 2
UNITS = 16
SCALE = float(HD) ** -0.5
EPS = 1e-5
BIAS_ROWS = 3 * 32
VALUES_AT = (4, 10, 15)
EXPERT_AT = (7, 9, 11, 13)
DMA = 16


def build(nc, x, ctx_in, g_xattn, g_ffn, Wq, bq, Wk, bk, Wv, bv, Wo, bo, wg, W, b_exp, out):
    es = ExitStack()
    with es:
        def sb(name, shape, dt=F32):
            return es.enter_context(nc.sbuf_tensor(name, shape, dt))

        def bank(name):
            return es.enter_context(nc.psum_tensor(name, [P, 512], F32))

        def sem(name):
            return es.enter_context(nc.semaphore(name))

        q_scr = [nc.dram_tensor(f"q_scr{i}", (SLOTS, P, SEQ), BF16, kind="Internal").ap() for i in range(2)]
        k_scr = [nc.dram_tensor(f"k_scr{i}", (SLOTS, P, SEQ), BF16, kind="Internal").ap() for i in range(2)]

        ident = sb("ident", [P, P])
        identb = sb("identb", [P, P], BF16)
        before = sb("before", [P, P], BF16)
        ones = sb("ones", [P, P], BF16)
        rank = sb("rank", [P, TILES, EXPERTS])
        minus_half = sb("minus_half", [P, TILES])
        w_raw = sb("w_raw", [P, 4, D])
        we_raw = sb("we_raw", [P, EXPERTS, D])
        wqT = sb("wqT", [P, 2, HD, PAIRS])
        wkT = sb("wkT", [P, 2, HD, PAIRS])
        wvT = sb("wvT", [P, D])
        woT = sb("woT", [P, D])
        weT = sb("weT", [P, EXPERTS, D])
        wg_sb = sb("wg_sb", [P, EXPERTS])
        bq_col = sb("bq_col", [P, 1])
        bk_col = sb("bk_col", [P, 1])
        bv_row = sb("bv_row", [P, D])
        bo_row = sb("bo_row", [P, D])
        gbo_row = sb("gbo_row", [P, D])
        be_sb = sb("be_sb", [BIAS_ROWS, D])
        be_rest = sb("be_rest", [BIAS_ROWS, 2, D])
        be_parts = sb("be_parts", [BIAS_ROWS, 3, D], BF16)
        be_stack = sb("be_stack", [BIAS_ROWS, D], BF16)
        gates = sb("gates", [P, 2])
        warm = sb("warm", [P, 1])
        tg = sb("tg", [P, 2])

        xin = [sb(f"xin{i}", [P, TILES, D]) for i in range(2)]
        cin = [sb(f"cin{i}", [P, TILES, D]) for i in range(2)]
        xres = [sb(f"xres{i}", [P, TILES, D]) for i in range(2)]
        stat1 = sb("stat1", [P, TILES, 6])
        mv1 = sb("mv1", [P, TILES, 2])
        var1 = sb("var1", [P, TILES])
        rstd1 = sb("rstd1", [P, TILES])
        xn = sb("xn", [P, TILES, D])
        frontT = [sb(f"frontT{i}", [P, 2, SEQ]) for i in range(2)]
        qk = sb("qk", [P, 2, SEQ])
        parts = sb("parts", [P, 3, 2, SEQ], BF16)
        rest = sb("rest", [P, 2, SEQ])
        qz = [sb(f"qz{i}", [P, 2, 2, HALF, SEQ], BF16) for i in range(2)]
        kst = [sb(f"kst{i}", [P, PAIRS, SEQ], BF16) for i in range(2)]
        vaug = [sb(f"vaug{i}", [P, TILES, H, 32]) for i in range(2)]
        negmax = sb("negmax", [P, 2, TILES, 2, HALF])
        mneg = sb("mneg", [P, 2, TILES, 2, 2 * HALF], BF16)
        mT = [sb(f"mT{i}", [4 * HALF, SEQ], BF16) for i in range(2)]
        probs = sb("probs", [P, UNITS, 2, SEQ])
        o_sb = sb("o_sb", [P, 2, SEQ])
        rsum = sb("rsum", [P, TILES * HALF * 2, 2])
        attn = sb("attn", [P, TILES, D])
        attnT = sb("attnT", [P, SEQ])
        x2 = [sb(f"x2_{i}", [P, TILES, D]) for i in range(2)]
        stat2 = sb("stat2", [P, TILES, 6])
        mv2 = sb("mv2", [P, TILES, 2])
        var2 = sb("var2", [P, TILES])
        rstd2 = sb("rstd2", [P, TILES])
        x2n = sb("x2n", [P, TILES, D])
        x2T = [sb(f"x2T{i}", [P, SEQ]) for i in range(2)]
        lmax = sb("lmax", [P, TILES])
        lsub = sb("lsub", [P, TILES, EXPERTS])
        lexp = sb("lexp", [P, TILES, EXPERTS])
        lsum = sb("lsum", [P, TILES])
        lrec = sb("lrec", [P, TILES])
        score = sb("score", [P, TILES, EXPERTS])
        smax = sb("smax", [P, TILES])
        chosen = sb("chosen", [P, TILES, EXPERTS], BF16)
        counts = sb("counts", [P, EXPERTS], BF16)
        gate = sb("gate", [P, TILES])
        kept = sb("kept", [P, TILES, EXPERTS])
        kept_b = sb("kept_b", [P, TILES, 3, 32], BF16)
        share = sb("share", [P, TILES, EXPERTS])
        keptT = sb("keptT", [BIAS_ROWS, SEQ], BF16)
        scaled = [sb(f"scaled{t}", [P, EXPERTS, D]) for t in range(TILES)]
        fold2, fold1 = sb("fold2", [P, 2, D]), sb("fold1", [P, D])
        first_sum = sb("first_sum", [P, TILES, D])
        tail4, tail2, tail1 = sb("tail4", [P, 4, D]), sb("tail2", [P, 2, D]), sb("tail1", [P, 1, D])
        base = sb("base", [P, TILES, D])
        res = sb("res", [P, NB * TILES, D])

        peak_ps = [bank("peak_ps0"), bank("peak_ps1")]
        st_ps = [bank("st_ps0"), bank("st_ps1")]
        o_ps = bank("o_ps")
        front_ps = bank("front_ps")
        post_ps = bank("post_ps")
        y_ps = bank("y_ps")
        front_b = front_ps[:, :].bitcast(BF16)

        x_in, c_in = [sem("x_in0"), sem("x_in1")], [sem("c_in0"), sem("c_in1")]
        xr_in = sem("xr_in")
        split_out = sem("split_out")
        stack_in = [sem("stack_in0"), sem("stack_in1")]
        max_in = [sem("max_in0"), sem("max_in1")]
        last_stored = sem("last_stored")
        stored = sem("stored")
        var1_ready, rstd1_ready, xn_ready = sem("var1_ready"), sem("rstd1_ready"), sem("xn_ready")
        frontT_mm, frontT_ready = sem("frontT_mm"), sem("frontT_ready")
        qk_mm, qk_ready = sem("qk_mm"), sem("qk_ready")
        part1_ready, rest_ready = sem("part1_ready"), sem("rest_ready")
        part2_ready, part3_ready = sem("part2_ready"), sem("part3_ready")
        v_mm, v_ready = sem("v_mm"), sem("v_ready")
        peak_mm, peak_read = sem("peak_mm"), sem("peak_read")
        hi_ready, mneg_ready = sem("hi_ready"), sem("mneg_ready")
        mT_mm, mT_ready = sem("mT_mm"), sem("mT_ready")
        st_mm, exp_ready = sem("st_mm"), sem("exp_ready")
        pv_mm = sem("pv_mm")
        o_ready, oT_mm, rsum_ready, attn_ready = sem("o_ready"), sem("oT_mm"), sem("rsum_ready"), sem("attn_ready")
        attnT_mm, attnT_ready, proj_mm = sem("attnT_mm"), sem("attnT_ready"), sem("proj_mm")
        xres_ready, x2_ready = sem("xres_ready"), sem("x2_ready")
        var2_ready, rstd2_ready, x2n_ready = sem("var2_ready"), sem("rstd2_ready"), sem("x2n_ready")
        x2T_mm, x2T_ready, logit_mm = sem("x2T_mm"), sem("x2T_ready"), sem("logit_mm")
        lsub_ready, lexp_ready, chosen_ready = sem("lsub_ready"), sem("lexp_ready"), sem("chosen_ready")
        gate_ready, loc_mm, kept_ready, share_ready = sem("gate_ready"), sem("loc_mm"), sem("kept_ready"), sem("share_ready")
        keptb_ready = sem("keptb_ready")
        keptT_mm, keptT_ready = sem("keptT_mm"), sem("keptT_ready")
        bias_mm, base_ready, y_mm, scaled_ready = sem("bias_mm"), sem("base_ready"), sem("y_mm"), sem("scaled_ready")
        folded, first_half = sem("folded"), sem("first_half")
        res_ready = sem("res_ready")
        stat1_done, mv1_done = sem("stat1_done"), sem("mv1_done")
        stat2_done, mv2_done = sem("stat2_done"), sem("mv2_done")
        lmax_done, score_done, smax_done = sem("lmax_done"), sem("score_done"), sem("smax_done")
        lsum_done, lrec_done, counts_done = sem("lsum_done"), sem("lrec_done"), sem("counts_done")
        tail = sem("tail")
        wqk_in, wvo_in, we_in, small_in = sem("wqk_in"), sem("wvo_in"), sem("we_in"), sem("small_in")
        bias_in, bexp_in, be_cleared = sem("bias_in"), sem("bexp_in"), sem("be_cleared")
        be_split, be_ready = sem("be_split"), sem("be_ready")
        ident_ready, const_ready, cleared, framed = sem("ident_ready"), sem("const_ready"), sem("cleared"), sem("framed")
        drawn, q_cleared = sem("drawn"), [sem("q_cleared0"), sem("q_cleared1")]
        wT_mm, wT_ready, weT_mm, weT_ready, tg_ready, gbo_ready = (
            sem("wT_mm"), sem("wT_ready"), sem("weT_mm"), sem("weT_ready"), sem("tg_ready"), sem("gbo_ready"))

        def wait(eng, s, batch, k=1, per=1, unit=1):
            if isinstance(batch, int):
                count = min(batch * per + k, NB * per)
                if count > 0:
                    eng.wait_ge(s, count * unit)
            else:
                eng.wait_ge(s, batch * (per * unit) + k * unit)

        def at(n, step):
            return isinstance(n, int) and n == step

        def live(batch):
            return not isinstance(batch, int) or 0 <= batch < NB

        def front_of(n, cur, two):
            if isinstance(n, int) and (n in (-1, 0) or not live(n + 2)):
                return None, None, None
            return n + 2, cur, two + 1

        def y_bank(batch, r):
            if isinstance(batch, int) and batch >= NB - 2:
                return (peak_ps + st_ps)[r if batch == NB - 2 else (r + 2) % 4]
            return y_ps

        def rows(ap, tile):
            return ap[:, bass.ds(tile, TILES), :]

        def tile_of(eng, batch):
            return batch * TILES if isinstance(batch, int) else eng.snap(batch * TILES)

        def steps(eng, step):
            for n in range(-2, 2):
                step(n, n % 2, n // 2)
            with eng.Fori(1, NB // 2 - 1) as two:
                step(two * 2, 0, two)
                step(two * 2 + 1, 1, two)
            for n in range(NB - 2, NB + 2):
                step(n, n % 2, n // 2)

        block = es.enter_context(nc.Block())

        @block.sync
        def _(sp):
            x_rows = x.rearrange("b (t p) d -> p (b t) d", p=P)
            c_rows = ctx_in.rearrange("b (t p) d -> p (b t) d", p=P)

            def load_first():
                sp.dma_start(xin[0][:], rows(x_rows, 0)).then_inc(x_in[0], DMA)
                sp.dma_start(cin[0][:], rows(c_rows, 0)).then_inc(c_in[0], DMA)
                for col, vector in ((bq_col, bq), (bk_col, bk)):
                    sp.dma_start(col[:], vector.rearrange("(p r d) -> r d p", r=2, d=HD),
                                 allow_slow_non_contiguous=True).then_inc(bias_in, DMA)
                sp.dma_start(xin[1][:], rows(x_rows, TILES)).then_inc(x_in[1], DMA)
                sp.dma_start(cin[1][:], rows(c_rows, TILES)).then_inc(c_in[1], DMA)
                sp.dma_start(w_raw[:, 2], Wv).then_inc(wvo_in, DMA)
                sp.dma_start(w_raw[:, 3], Wo).then_inc(wvo_in, DMA)
                sp.dma_start(we_raw[:], W.rearrange("e f h -> f e h")).then_inc(we_in, DMA)
                wait(sp, xn_ready, 0)
                sp.dma_start(xin[0][:], rows(x_rows, 2 * TILES)).then_inc(x_in[0], DMA)
                wait(sp, frontT_mm, 0)
                sp.dma_start(cin[0][:], rows(c_rows, 2 * TILES)).then_inc(c_in[0], DMA)
                sp.dma_start(gates[:, 0:1], g_xattn.unsqueeze(0).broadcast_to([P, 1])).then_inc(small_in, DMA)
                sp.dma_start(gates[:, 1:2], g_ffn.unsqueeze(0).broadcast_to([P, 1])).then_inc(small_in, DMA)
                sp.dma_start(bv_row[:], bv.unsqueeze(0).broadcast_to([P, D])).then_inc(small_in, DMA)
                sp.dma_start(bo_row[:], bo.unsqueeze(0).broadcast_to([P, D])).then_inc(small_in, DMA)
                sp.dma_start(wg_sb[:], wg).then_inc(small_in, DMA)
                sp.wait_ge(be_cleared, 1)
                for i in range(3):
                    sp.dma_start(be_sb[32 * i:32 * i + EXPERTS], b_exp).then_inc(bexp_in, DMA)

            def load_stack(batch, par, half):
                wait(sp, st_mm, batch - 2, UNITS // 2 * (half + 1), UNITS)
                wait(sp, split_out, batch, 6, 6, DMA)
                if isinstance(batch, int) and batch < 2:
                    sp.wait_ge(cleared, 2)
                    sp.wait_ge(q_cleared[par], 1)
                pairs = slice(half * HALF, (half + 1) * HALF)
                for r in range(2):
                    for dst, scr in ((kst[par][r * HROWS:(r + 1) * HROWS, pairs, :], k_scr[par]),
                                     (qz[par][r * HROWS:(r + 1) * HROWS, half, r, :, :], q_scr[par])):
                        src = scr.rearrange("s (r d p) q -> r s d p q", r=2, d=HD)[r, :, :, pairs, :]
                        sp.dma_start(dst, src.rearrange("s d p q -> s d (p q)")).then_inc(stack_in[half], DMA)

            def store_parts(batch, par):
                for part, ready, q_slots, k_slots in (
                        (0, part1_ready, slice(0, 3), slice(1, 6, 2)),
                        (1, part2_ready, slice(3, 5), slice(2, 5, 2)),
                        (2, part3_ready, slice(5, 6), slice(0, 1))):
                    wait(sp, ready, batch)
                    for t, scr, slots in ((0, q_scr[par], q_slots), (1, k_scr[par], k_slots)):
                        dst = scr[slots].rearrange("s z q -> z s q")
                        src = parts[:, part, t, :].unsqueeze(1).broadcast_to(list(dst.shape))
                        sp.dma_start(dst, src).then_inc(split_out, DMA)

            def load_max(batch, par, half):
                wait(sp, mT_ready, batch, half + 1, 2)
                sp.dma_start(qz[par][QROWS:KROWS, half].rearrange("a r p q -> a (r p) q"),
                             mT[half][:]).then_inc(max_in[half], DMA)

            def step(n, cur, two):
                nxt = 1 - cur
                front, par, pair = front_of(n, cur, two)
                front_tile = None if front is None else tile_of(sp, front)
                attend_tile = tile_of(sp, n)
                if at(n, -2):
                    load_first()
                elif front is not None:
                    wait(sp, xn_ready, front - 2)
                    sp.dma_start(xin[par][:], rows(x_rows, front_tile)).then_inc(x_in[par], DMA)
                    wait(sp, frontT_mm, front - 2)
                    sp.dma_start(cin[par][:], rows(c_rows, front_tile)).then_inc(c_in[par], DMA)
                if live(n + 1):
                    load_stack(n + 1, nxt, 1)
                if live(n):
                    wait(sp, x2_ready, n - 2)
                    wait(sp, xres_ready, n - 1)
                    sp.dma_start(xres[cur][:], rows(x_rows, attend_tile)).then_inc(xr_in, DMA)
                    load_max(n, cur, 1)
                if at(n, -1):
                    store_parts(1, 1)
                    sp.wait_ge(peak_mm, 1)
                    load_stack(1, 1, 0)
                    load_max(0, 0, 0)
                    sp.wait_ge(stack_in[1], 4 * DMA)
                    store_parts(2, 0)
                else:
                    if front is not None:
                        store_parts(front, par)
                    if live(n + 1):
                        load_max(n + 1, nxt, 0)
                    if live(n + 2):
                        load_stack(n + 2, cur, 0)

            steps(sp, step)

        @block.gpsimd
        def _(pool):
            o_rows = out.rearrange("b (t p) d -> p (b t) d", p=P)
            nc.gpsimd.memset(ident[:], 0.0).then_inc(drawn, 1)
            pool.wait_ge(drawn, 1)
            nc.gpsimd.affine_select(out=ident[:], in_=ident[:], compare_op=ALU.not_equal, fill=1.0, base=0,
                                    pattern=[[-1, P]], channel_multiplier=1).then_inc(ident_ready, 1)
            nc.gpsimd.memset(minus_half[:], -0.5).then_inc(ident_ready, 1)
            nc.gpsimd.memset(be_sb[:], 0.0).then_inc(be_cleared, 1)
            def constants():
                for i in range(2):
                    nc.gpsimd.memset(kst[i][:], 1.0).then_inc(cleared, 1)

            def more_constants():
                nc.gpsimd.memset(ones[:], 1.0).then_inc(drawn, 1)
                pool.wait_ge(ident_ready, 2)
                nc.gpsimd.tensor_copy(identb[:], ident[:]).then_inc(const_ready, 1)
                pool.wait_ge(drawn, 2)
                nc.gpsimd.affine_select(out=before[:], in_=ones[:], compare_op=ALU.is_gt, fill=0.0, base=0,
                                        pattern=[[1, P]], channel_multiplier=-1).then_inc(const_ready, 1)
                for e in range(EXPERTS):
                    nc.gpsimd.memset(rank[:, :, e:e + 1], float(EXPERTS - e)).then_inc(const_ready, 1)

            def split_bias():
                pool.wait_ge(bexp_in, 3 * DMA)
                left = (be_sb[:], be_rest[:, 0], be_rest[:, 1])
                for i in range(3):
                    nc.gpsimd.tensor_copy(be_parts[:, i], left[i]).then_inc(be_split, 1)
                    pool.wait_ge(be_split, 2 * i + 1)
                    if i < 2:
                        nc.gpsimd.tensor_tensor(left[i + 1], left[i], be_parts[:, i], ALU.subtract).then_inc(be_split, 1)
                        pool.wait_ge(be_split, 2 * i + 2)
                for i in range(3):
                    nc.gpsimd.tensor_copy(be_stack[32 * i:32 * i + 32], be_parts[32 * i:32 * i + 32, i]).then_inc(be_ready, 1)

            def front_root(batch):
                if at(batch, 0):
                    pool.wait_ge(ident_ready, 2)
                wait(pool, var1_ready, batch)
                nc.gpsimd.tensor_tensor(rstd1[:], var1[:], minus_half[:], ALU.pow).then_inc(rstd1_ready, 1)

            def split(batch):
                wait(pool, part1_ready, batch)
                wait(pool, part2_ready, batch - 1)
                nc.gpsimd.tensor_tensor(rest[:], qk[:], parts[:, 0], ALU.subtract).then_inc(rest_ready, 1)
                wait(pool, part2_ready, batch)
                wait(pool, split_out, batch - 1, 6, 6, DMA)
                nc.gpsimd.tensor_tensor(parts[:, 2], rest[:], parts[:, 1], ALU.subtract).then_inc(part3_ready, 1)

            def fold(batch, r):
                t, half = r // 2, r % 2
                wait(pool, scaled_ready, batch, r + 1, 4)
                nc.gpsimd.tensor_tensor(fold2[:], scaled[t][:, 4 * half:4 * half + 2],
                                        scaled[t][:, 4 * half + 2:4 * half + 4], ALU.add).then_inc(folded, 1)
                wait(pool, folded, batch, 2 * r + 1, 8)
                nc.gpsimd.tensor_tensor(fold1[:], fold2[:, 0], fold2[:, 1], ALU.add).then_inc(folded, 1)
                wait(pool, folded, batch, 2 * r + 2, 8)
                if half == 0:
                    wait(pool, base_ready, batch)
                    nc.gpsimd.tensor_tensor(first_sum[:, t], fold1[:], base[:, t], ALU.add).then_inc(first_half, 1)
                else:
                    wait(pool, first_half, batch, t + 1, TILES)
                    nc.gpsimd.tensor_tensor(rows(res[:], batch * TILES)[:, t], fold1[:], first_sum[:, t],
                                            ALU.add).then_inc(res_ready, 1)

            def step(n, cur, two):
                nxt = 1 - cur
                expert_tile = tile_of(pool, n - 2)
                front, par, pair = front_of(n, cur, two)
                if at(n, -1):
                    split(1)
                elif front is not None:
                    front_root(front)
                if live(n - 1):
                    wait(pool, xr_in, n - 1, 1, 1, DMA)
                    if isinstance(n, int):
                        pool.wait_ge(gbo_ready, 1)
                    nc.gpsimd.tensor_tensor(xres[nxt][:], xres[nxt][:],
                                            gbo_row[:].unsqueeze(1).broadcast_to([P, TILES, D]),
                                            ALU.add).then_inc(xres_ready, 1)
                if at(n, -2):
                    front_root(1)
                    constants()
                    front_root(2)
                    more_constants()
                if at(n, -1):
                    split(2)
                if front is not None and not at(n, -2):
                    split(front)
                if at(n, -1):
                    split_bias()
                if live(n - 1):
                    wait(pool, var2_ready, n - 1)
                    nc.gpsimd.tensor_tensor(rstd2[:], var2[:], minus_half[:], ALU.pow).then_inc(rstd2_ready, 1)
                if live(n - 2):
                    last = at(n, NB + 1)
                    for r in range(2 if last else 4):
                        fold(n - 2, r)
                if live(n - 2) and not last:
                    wait(pool, res_ready, n - 2, 2, 2)
                    pool.dma_start(rows(o_rows, expert_tile), rows(res[:], expert_tile)).then_inc(stored, DMA)

            steps(pool, step)
            pool.wait_ge(stored, (NB - 1) * DMA)

        @block.scalar
        def _(act):
            act.dma_start(w_raw[:, 0], Wq).then_inc(wqk_in, DMA)
            act.dma_start(w_raw[:, 1], Wk).then_inc(wqk_in, DMA)
            act.wait_ge(ident_ready, 1)
            nc.scalar.activation(warm[:], ident[:, 0:1], ACT.Exp)
            act.wait_ge(wT_mm, 2)
            nc.scalar.copy(wqT[:], front_ps[:, 0:D].rearrange("z (p r d) -> z r d p", r=2, d=HD)).then_inc(wT_ready, 1)
            nc.scalar.copy(wkT[:], front_ps[:, D:2 * D].rearrange("z (p r d) -> z r d p", r=2, d=HD)).then_inc(wT_ready, 1)
            act.wait_ge(bias_in, 2 * DMA)

            def late_setup():
                act.wait_ge(wT_mm, 4)
                nc.scalar.copy(wvT[:], post_ps[:, 0:D]).then_inc(wT_ready, 1)
                nc.scalar.copy(woT[:], post_ps[:, D:2 * D]).then_inc(wT_ready, 1)
                for half in range(2):
                    act.wait_ge(weT_mm, half + 1)
                    nc.scalar.copy(weT[:, 4 * half:4 * half + 4, :], st_ps[half][:]).then_inc(weT_ready, 1)
                act.wait_ge(small_in, 5 * DMA)
                nc.scalar.activation(tg[:], gates[:], ACT.Tanh).then_inc(tg_ready, 1)

            def copy_max(batch, half):
                wait(act, mT_mm, batch, half + 1, 2)
                wait(act, max_in[half], batch - 1, 1, 1, DMA)
                nc.scalar.copy(mT[half][:], front_b[0:4 * HALF, 0:SEQ]).then_inc(mT_ready, 1)

            def copy_front(batch, par):
                wait(act, frontT_mm, batch)
                nc.scalar.copy(frontT[par][:], front_ps[:]).then_inc(frontT_ready, 1)

            def copy_qk(batch):
                wait(act, qk_mm, batch)
                wait(act, rest_ready, batch - 1)
                for t, bias in ((0, bq_col), (1, bk_col)):
                    last = nc.scalar.activation(qk[:, t], front_ps[:, t * SEQ:(t + 1) * SEQ], ACT.Identity,
                                                bias=bias[:, 0:1])
                last.then_inc(qk_ready, 1)

            def first_part(batch):
                wait(act, qk_ready, batch)
                wait(act, split_out, batch - 1, 6, 6, DMA)
                nc.scalar.copy(parts[:, 0], qk[:]).then_inc(part1_ready, 1)

            def scale(batch, r):
                t, first = r // 2, 4 * (r % 2)
                last = at(batch, NB - 1)
                wait(act, y_mm, batch, r + 3 if last else r + 1, 4)
                if r == 0:
                    wait(act, share_ready, batch)
                if isinstance(batch, int):
                    wait(act, folded, batch - 1, 2 * r + 1, 8)
                for i in range(4):
                    last = nc.scalar.activation(scaled[t][:, first + i], y_bank(batch, r)[:, i * D:(i + 1) * D], ACT.Copy,
                                                scale=share[:, t, first + i:first + i + 1])
                last.then_inc(scaled_ready, 1)

            def step(n, cur, two):
                nxt = 1 - cur
                front, par, pair = front_of(n, cur, two)
                if at(n, -1):
                    copy_front(1, 1)
                    copy_qk(1)
                    copy_front(2, 0)
                    first_part(1)
                    copy_qk(2)
                for s in range(UNITS):
                    if live(n):
                        wait(act, st_mm, n, s + 1, UNITS)
                        wait(act, pv_mm, n - 1, s // 4 + 1, 4)
                        nc.scalar.activation(probs[:, s], st_ps[s % 2][:], ACT.Exp,
                                             scale=SCALE).then_inc(exp_ready, 1)
                    if s == 3 and live(n):
                        copy_max(n, 1)
                    if s == 1 and live(n - 1):
                        wait(act, pv_mm, n - 1, 4, 4)
                        wait(act, oT_mm, n - 2)
                        nc.scalar.copy(o_sb[:], o_ps[:]).then_inc(o_ready, 1)
                    if s == 3 and live(n - 2):
                        wait(act, keptT_mm, n - 2)
                        nc.scalar.copy(keptT[:], y_ps[:, :].bitcast(BF16)[0:BIAS_ROWS, 0:SEQ]).then_inc(keptT_ready, 1)
                    if s == 4 and front is not None:
                        copy_front(front, par)
                    if s == 6 and live(n - 1):
                        wait(act, attnT_mm, n - 1)
                        nc.scalar.copy(attnT[:], post_ps[:, 0:SEQ]).then_inc(attnT_ready, 1)
                    if s == 6 and front is not None:
                        copy_qk(front)
                    if s == 6 and front is not None and not at(n, -2):
                        first_part(front)
                    if s in EXPERT_AT and live(n - 2):
                        r = EXPERT_AT.index(s)
                        if not (at(n, NB + 1) and r >= 2):
                            scale(n - 2, r)
                    if s == 9 and live(n + 1):
                        copy_max(n + 1, 0)
                    if s == 9 and at(n, -1):
                        first_part(2)
                    if s == 11 and live(n - 1):
                        wait(act, x2T_mm, n - 1)
                        nc.scalar.copy(x2T[nxt][:], post_ps[:, 0:SEQ]).then_inc(x2T_ready, 1)
                    if s == 15 and live(n - 1):
                        wait(act, lsub_ready, n - 1)
                        nc.scalar.activation(lexp[:], lsub[:], ACT.Exp).then_inc(lexp_ready, 1)
                if at(n, -2):
                    late_setup()

            steps(act, step)
            wait(act, res_ready, NB - 1, 2, 2)
            act.dma_start(out.rearrange("b (t p) d -> p (b t) d", p=P)[:, (NB - 1) * TILES:],
                          res[:, (NB - 1) * TILES:]).then_inc(last_stored, DMA)
            act.wait_ge(last_stored, DMA)

        @block.vector
        def _(dve):
            def peak(batch, s):
                half, p, r = s // 8, (s % 8) // 2, s % 2
                wait(dve, peak_mm, batch, s + 1, UNITS)
                nc.vector.tensor_reduce(negmax[:, half, :, r, p], peak_ps[s % 2][:].rearrange("z (t k) -> z t k", t=TILES),
                                        axis=AX.X, op=ALU.max, negate=True).then_inc(peak_read, 1)

            def max_high(batch, half):
                wait(dve, peak_read, batch, 8 * (half + 1), UNITS)
                nc.vector.tensor_copy(mneg[:, half, :, 0, :],
                                      negmax[:, half].rearrange("z t r p -> z t (r p)")).then_inc(hi_ready, 1)

            def max_low(batch, half):
                wait(dve, hi_ready, batch, half + 1, 2)
                nc.vector.tensor_tensor(mneg[:, half, :, 1, :], negmax[:, half].rearrange("z t r p -> z t (r p)"),
                                        mneg[:, half, :, 0, :], ALU.subtract).then_inc(mneg_ready, 1)

            def statistics(src, stat, stat_done):
                for t in range(TILES):
                    last = nc.vector.bn_stats(stat[:, t], src[:, t])
                last.then_inc(stat_done, 1)

            def variance(batch, stat, mv, var, mv_done, var_ready):
                for t in range(TILES):
                    last = nc.vector.bn_aggr(mv[:, t], stat[:, t])
                last.then_inc(mv_done, 1)
                wait(dve, mv_done, batch)
                nc.vector.tensor_scalar(var[:], mv[:, :, 1], EPS, None, ALU.add).then_inc(var_ready, 1)

            def norm(dst, src, mv, rstd, ready):
                for t in range(TILES):
                    last = nc.vector.tensor_scalar(dst[:, t], src[:, t], mv[:, t, 0:1], rstd[:, t:t + 1],
                                                   ALU.subtract, ALU.mult)
                last.then_inc(ready, 1)

            def front_norm(batch, par):
                wait(dve, rstd1_ready, batch)
                wait(dve, frontT_mm, batch - 1)
                norm(xn, xin[par], mv1, rstd1, xn_ready)

            def second_part(batch):
                wait(dve, rest_ready, batch)
                nc.vector.tensor_copy(parts[:, 1], rest[:]).then_inc(part2_ready, 1)

            def place_v(batch, par):
                wait(dve, v_mm, batch)
                wait(dve, pv_mm, batch - 2, 4, 4)
                if at(batch, 0):
                    dve.wait_ge(small_in, 5 * DMA)
                v_ps = post_ps if at(batch, 0) else front_ps
                for t in range(TILES):
                    dst = vaug[par][:, t].rearrange("z (p r) c -> z p (r c)", r=2)
                    for r in range(2):
                        last = nc.vector.tensor_tensor(
                            dst[:, :, r * (32 + HD):r * (32 + HD) + HD],
                            v_ps[:, t * D:(t + 1) * D].rearrange("z (p r d) -> z r p d", r=2, d=HD)[:, r],
                            bv_row[:].rearrange("z (p r d) -> z r p d", r=2, d=HD)[:, r], ALU.add)
                last.then_inc(v_ready, 1)

            def normalise(batch):
                wait(dve, oT_mm, batch)
                oT = post_ps[:].rearrange("z (g c) -> z g c", c=32)
                nc.vector.reciprocal(rsum[:], oT[:, :, 2 * HD:2 * HD + 2]).then_inc(rsum_ready, 1)
                wait(dve, rsum_ready, batch)
                wait(dve, attnT_mm, batch - 1)
                nc.vector.tensor_tensor(
                    attn[:].rearrange("z t (g r d) -> z (t g) r d", r=2, d=HD),
                    oT[:, :, 0:2 * HD].rearrange("z g (r d) -> z g r d", r=2),
                    rsum[:].unsqueeze(3).broadcast_to([P, TILES * PAIRS, 2, HD]), ALU.mult).then_inc(attn_ready, 1)

            def residual(batch, par):
                wait(dve, proj_mm, batch)
                wait(dve, xres_ready, batch)
                nc.vector.scalar_tensor_tensor(x2[par][:].rearrange("z t d -> z (t d)"), post_ps[:, 0:SEQ], tg[:, 0:1],
                                               xres[par][:].rearrange("z t d -> z (t d)"),
                                               ALU.mult, ALU.add).then_inc(x2_ready, 1)
                wait(dve, x2_ready, batch)
                statistics(x2[par], stat2, stat2_done)

            def choose(batch):
                wait(dve, logit_mm, batch)
                logits = post_ps[:, 0:TILES * EXPERTS].rearrange("z (t e) -> z t e", t=TILES)
                nc.vector.tensor_reduce(lmax[:], logits, axis=AX.X, op=ALU.max).then_inc(lmax_done, 1)
                wait(dve, lmax_done, batch)
                nc.vector.tensor_tensor(lsub[:], logits, lmax[:].unsqueeze(2).broadcast_to([P, TILES, EXPERTS]),
                                        ALU.subtract).then_inc(lsub_ready, 1)
                wait(dve, lsub_ready, batch)
                nc.vector.scalar_tensor_tensor(score[:], lsub[:], 0.0, rank[:], ALU.is_ge, ALU.mult).then_inc(score_done, 1)
                wait(dve, score_done, batch)
                nc.vector.tensor_reduce(smax[:], score[:], axis=AX.X, op=ALU.max).then_inc(smax_done, 1)
                wait(dve, smax_done, batch)
                nc.vector.tensor_tensor(chosen[:], score[:], smax[:].unsqueeze(2).broadcast_to([P, TILES, EXPERTS]),
                                        ALU.is_equal).then_inc(chosen_ready, 1)

            def total(batch):
                wait(dve, lexp_ready, batch)
                nc.vector.tensor_reduce(lsum[:], lexp[:], axis=AX.X, op=ALU.add).then_inc(lsum_done, 1)

            def invert(batch):
                wait(dve, lsum_done, batch)
                nc.vector.reciprocal(lrec[:], lsum[:]).then_inc(lrec_done, 1)

            def gate_tokens(batch):
                wait(dve, lrec_done, batch)
                nc.vector.tensor_scalar(gate[:], lrec[:], tg[:, 1:2], None, ALU.mult).then_inc(gate_ready, 1)

            def keep(batch, par):
                wait(dve, loc_mm, batch)
                loc = post_ps[:, 0:TILES * EXPERTS].rearrange("z (t e) -> z t e", t=TILES)
                nc.vector.scalar_tensor_tensor(kept[:], loc, float(CAPACITY), chosen[:],
                                               ALU.is_lt, ALU.mult).then_inc(kept_ready, 1)
                nc.vector.tensor_tensor(counts[:], counts[:], chosen[:, 0], ALU.add).then_inc(counts_done, 1)
                wait(dve, kept_ready, batch)
                nc.vector.tensor_copy(kept_b[:, :, :, 0:EXPERTS],
                                      kept[:].unsqueeze(2).broadcast_to([P, TILES, 3, EXPERTS])).then_inc(keptb_ready, 1)
                wait(dve, gate_ready, batch)
                nc.vector.tensor_tensor(share[:], kept[:], gate[:].unsqueeze(2).broadcast_to([P, TILES, EXPERTS]),
                                        ALU.mult).then_inc(share_ready, 1)
                wait(dve, counts_done, batch, 1, TILES)
                nc.vector.tensor_tensor(counts[:], counts[:], chosen[:, 1], ALU.add).then_inc(counts_done, 1)

            def take_base(batch, par):
                wait(dve, bias_mm, batch)
                if isinstance(batch, int):
                    wait(dve, res_ready, batch - 1, 2, 2)
                for t in range(TILES):
                    last = nc.vector.scalar_tensor_tensor(base[:, t], y_ps[:, t * D:(t + 1) * D], gate[:, t:t + 1],
                                                          x2[par][:, t], ALU.mult, ALU.add)
                last.then_inc(base_ready, 1)

            def clear_stack(i):
                nc.vector.memset(qz[i][:].rearrange("z h r p q -> z (h r p q)").bitcast(mybir.dt.uint32), 0).then_inc(q_cleared[i], 1)

            def clear():
                for i in range(2):
                    nc.vector.memset(vaug[i][:], 0.0).then_inc(framed, 1)
                nc.vector.memset(counts[:], 0.0)
                nc.vector.memset(kept_b[:], 0.0)
                dve.wait_ge(framed, 2)
                for i in range(2):
                    frame = vaug[i][:].rearrange("z t (p r) c -> z t p (r c)", r=2)
                    for r in range(2):
                        column = r * 32 + 2 * HD + r
                        nc.vector.memset(frame[:, :, :, column:column + 1], 1.0)

            def early_norm(batch):
                par = batch % 2
                wait(dve, x_in[par], batch // 2, 1, 1, DMA)
                statistics(xin[par], stat1, stat1_done)
                wait(dve, stat1_done, batch)
                variance(batch, stat1, mv1, var1, mv1_done, var1_ready)
                front_norm(batch, par)

            def first_split():
                wait(dve, qk_ready, 0)
                nc.vector.tensor_copy(parts[:, 0], qk[:]).then_inc(part1_ready, 1)
                wait(dve, part1_ready, 0)
                nc.vector.tensor_tensor(rest[:], qk[:], parts[:, 0], ALU.subtract).then_inc(rest_ready, 1)
                wait(dve, rest_ready, 0)
                nc.vector.tensor_copy(parts[:, 1], rest[:]).then_inc(part2_ready, 1)
                wait(dve, part2_ready, 0)
                nc.vector.tensor_tensor(parts[:, 2], rest[:], parts[:, 1], ALU.subtract).then_inc(part3_ready, 1)

            def last_tile():
                batch, t = NB - 1, 1
                wait(dve, share_ready, batch)
                for r in (2, 3):
                    first = 4 * (r % 2)
                    wait(dve, y_mm, batch, r - 1, 4)
                    wait(dve, folded, batch - 1, 2 * r + 1, 8)
                    nc.vector.tensor_tensor(scaled[t][:, first:first + 4],
                                            y_bank(batch, r)[:].rearrange("z (e d) -> z e d", e=4),
                                            share[:, t, first:first + 4].unsqueeze(2).broadcast_to([P, 4, D]),
                                            ALU.mult).then_inc(tail, 1)
                take_base(batch, batch % 2)
                steps_of = ((tail4, scaled[t][:, 0:4], scaled[t][:, 4:8]), (tail2, tail4[:, 0:2], tail4[:, 2:4]),
                            (tail1, tail2[:, 0:1], tail2[:, 1:2]))
                for i, (dst, a, b) in enumerate(steps_of):
                    dve.wait_ge(tail, 2 + i)
                    nc.vector.tensor_tensor(dst[:], a, b, ALU.add).then_inc(tail, 1)
                dve.wait_ge(tail, 5)
                wait(dve, base_ready, batch)
                nc.vector.tensor_tensor(rows(res[:], batch * TILES)[:, t], tail1[:, 0], base[:, t],
                                        ALU.add).then_inc(res_ready, 1)

            def gated_bias():
                dve.wait_ge(small_in, 5 * DMA)
                dve.wait_ge(tg_ready, 1)
                nc.vector.tensor_scalar(gbo_row[:], bo_row[:], tg[:, 0:1], None, ALU.mult).then_inc(gbo_ready, 1)

            def step(n, cur, two):
                nxt = 1 - cur
                if at(n, -1):
                    second_part(1)
                    place_v(0, 0)
                front, par, pair = front_of(n, cur, two)
                if at(n, -2):
                    clear_stack(0)
                if live(n):
                    max_high(n, 1)
                if live(n - 2):
                    total(n - 2)
                if live(n):
                    max_low(n, 1)
                if live(n - 2):
                    invert(n - 2)
                for s in range(UNITS):
                    if s == 9 and live(n - 1):
                        wait(dve, stat2_done, n - 1)
                    if s == 1 and front is not None:
                        wait(dve, stat1_done, front)
                    if live(n + 1):
                        peak(n + 1, s)
                    if s == 0 and live(n - 2):
                        gate_tokens(n - 2)
                    if s == 0 and front is not None:
                        wait(dve, x_in[par], pair, 1, 1, DMA)
                        statistics(xin[par], stat1, stat1_done)
                    if s == 1 and front is not None:
                        variance(front, stat1, mv1, var1, mv1_done, var1_ready)
                    if s == 1 and live(n - 2):
                        keep(n - 2, cur)
                    if s == 2 and front is not None:
                        front_norm(front, par)
                        if at(n, -2):
                            early_norm(1)
                            clear()
                            first_split()
                            early_norm(2)
                            clear_stack(1)
                    if s == 4 and live(n - 1):
                        normalise(n - 1)
                    if s == 5 and live(n - 2) and not at(n, NB + 1):
                        take_base(n - 2, cur)
                    if s == 7 and live(n + 1):
                        max_high(n + 1, 0)
                        max_low(n + 1, 0)
                    if s == 8 and live(n - 1):
                        residual(n - 1, nxt)
                    if s == 13 and at(n, -1):
                        second_part(2)
                    if s == 8 and front is not None and not at(n, -2):
                        second_part(front)
                    if s == 9 and live(n - 1):
                        variance(n - 1, stat2, mv2, var2, mv2_done, var2_ready)
                    if s == 10 and live(n - 1):
                        wait(dve, rstd2_ready, n - 1)
                        wait(dve, x2T_mm, n - 2)
                        norm(x2n, x2[nxt], mv2, rstd2, x2n_ready)
                    if s == 12 and live(n + 1) and not at(n, -1):
                        place_v(n + 1, nxt)
                    if s == 13 and live(n - 1):
                        choose(n - 1)
                if at(n, NB + 1):
                    last_tile()
                if at(n, -2):
                    gated_bias()

            steps(dve, step)

        @block.tensor
        def _(pe):
            def turn_weights(pairs, ready):
                for dst, src in pairs:
                    last = nc.tensor.transpose(dst, src, ident[:])
                last.then_inc(ready, 1)

            pe.wait_ge(ident_ready, 1)
            pe.wait_ge(wqk_in, 2 * DMA)
            turn_weights([(front_ps[:, 0:D], w_raw[:, 0])], wT_mm)
            turn_weights([(front_ps[:, D:2 * D], w_raw[:, 1])], wT_mm)
            pe.wait_ge(wT_ready, 2)

            def late_setup():
                pe.wait_ge(wvo_in, 2 * DMA)
                turn_weights([(post_ps[:, 0:D], w_raw[:, 2])], wT_mm)
                turn_weights([(post_ps[:, D:2 * D], w_raw[:, 3])], wT_mm)
                pe.wait_ge(we_in, DMA)
                for half in range(2):
                    turn_weights([(st_ps[half][:, i * D:(i + 1) * D], we_raw[:, 4 * half + i]) for i in range(4)], weT_mm)

            def peak(batch, par, s):
                half, p, r = s // 8, s // 2, s % 2
                if s % 8 == 0:
                    wait(pe, stack_in[half], batch, 4, 4, DMA)
                wait(pe, peak_read, batch, s - 1, UNITS)
                for t in range(TILES):
                    last = nc.tensor.matmul(peak_ps[s % 2][:, t * SEQ:(t + 1) * SEQ],
                                            qz[par][0:QROWS, half, r, p % HALF, t * P:(t + 1) * P], kst[par][0:QROWS, p, :],
                                            start=True, stop=True)
                last.then_inc(peak_mm, 1)

            def scores(batch, par, s):
                half, t, g = s // 8, (s % 8) // 4, s % 4
                p = half * HALF + g
                if s % 8 == 0:
                    wait(pe, max_in[half], batch, 1, 1, DMA)
                wait(pe, exp_ready, batch, s - 1, UNITS)
                nc.tensor.matmul(st_ps[s % 2][:], kst[par][0:KROWS, p, t * P:(t + 1) * P], qz[par][0:KROWS, half, :, g, :],
                                 start=True, stop=True).then_inc(st_mm, 1)

            def values(batch, par, quarter):
                half, t = quarter // 2, quarter % 2
                wait(pe, exp_ready, batch, 4 * quarter + 4, UNITS)
                if quarter == 0:
                    wait(pe, v_ready, batch)
                    wait(pe, o_ready, batch - 1)
                for r in range(2):
                    for g in range(4):
                        last = nc.tensor.matmul(o_ps[32 * g:32 * g + 32, half * SEQ:(half + 1) * SEQ],
                                                vaug[par][:, t, 2 * (half * HALF + g) + r, :],
                                                probs[:, 4 * quarter + g, r, :],
                                                start=(t == 0 and r == 0), stop=(t == 1 and r == 1))
                last.then_inc(pv_mm, 1)

            def turn_max(batch, half):
                if isinstance(batch, int) and batch < 2:
                    wait(pe, qk_ready, 2)
                    wait(pe, mT_ready, 0, 1 + batch - (half == 0 and batch == 0), 2)
                if half == 0:
                    wait(pe, qk_ready, batch + 1)
                else:
                    wait(pe, v_ready, batch)
                wait(pe, mneg_ready, batch, half + 1, 2)
                for t in range(TILES):
                    last = nc.tensor.transpose(front_b[0:4 * HALF, t * P:(t + 1) * P],
                                               mneg[:, half, t].rearrange("z a h -> z (a h)"), identb[:])
                last.then_inc(mT_mm, 1)

            def turn_front(batch, par, two):
                if isinstance(batch, int) and batch in (1, 2):
                    wait(pe, qk_ready, batch - 1)
                else:
                    wait(pe, mT_ready, batch - 2, 2, 2)
                wait(pe, xn_ready, batch)
                wait(pe, c_in[par], two, 1, 1, DMA)
                for i, src in ((0, xn), (1, cin[par])):
                    for t in range(TILES):
                        last = nc.tensor.transpose(front_ps[:, i * SEQ + t * P:i * SEQ + (t + 1) * P], src[:, t], ident[:])
                last.then_inc(frontT_mm, 1)

            def project_qk(batch, par):
                wait(pe, frontT_ready, batch)
                for i, w in ((0, wqT), (1, wkT)):
                    last = nc.tensor.matmul(front_ps[:, i * SEQ:(i + 1) * SEQ], w[:].rearrange("z r d p -> z (r d p)"),
                                            frontT[par][:, i], start=True, stop=True)
                last.then_inc(qk_mm, 1)

            def project_v(batch, par):
                if at(batch, 0):
                    pe.wait_ge(wT_ready, 4)
                    v_ps = post_ps
                else:
                    wait(pe, mT_ready, batch, 1, 2)
                    v_ps = front_ps
                for t in range(TILES):
                    last = nc.tensor.matmul(v_ps[:, t * D:(t + 1) * D], frontT[par][:, 1, t * P:(t + 1) * P], wvT[:],
                                            start=True, stop=True)
                last.then_inc(v_mm, 1)

            def turn_o(batch):
                wait(pe, o_ready, batch)
                wait(pe, kept_ready, batch - 1)
                for t in range(TILES):
                    for half in range(2):
                        last = nc.tensor.transpose(post_ps[:, (t * 2 + half) * P:(t * 2 + half + 1) * P],
                                                   o_sb[:, half, t * P:(t + 1) * P], ident[:])
                last.then_inc(oT_mm, 1)

            def turn_attn(batch):
                wait(pe, attn_ready, batch)
                for t in range(TILES):
                    last = nc.tensor.transpose(post_ps[:, t * P:(t + 1) * P], attn[:, t], ident[:])
                last.then_inc(attnT_mm, 1)

            def project_o(batch):
                wait(pe, attnT_ready, batch)
                for t in range(TILES):
                    last = nc.tensor.matmul(post_ps[:, t * D:(t + 1) * D], attnT[:, t * P:(t + 1) * P], woT[:],
                                            start=True, stop=True)
                last.then_inc(proj_mm, 1)

            def turn_x2(batch):
                wait(pe, x2n_ready, batch)
                for t in range(TILES):
                    last = nc.tensor.transpose(post_ps[:, t * P:(t + 1) * P], x2n[:, t], ident[:])
                last.then_inc(x2T_mm, 1)

            def route(batch, par):
                wait(pe, x2T_ready, batch)
                for t in range(TILES):
                    last = nc.tensor.matmul(post_ps[:, t * EXPERTS:(t + 1) * EXPERTS], x2T[par][:, t * P:(t + 1) * P],
                                            wg_sb[:], start=True, stop=True)
                last.then_inc(logit_mm, 1)

            def locate(batch):
                wait(pe, chosen_ready, batch)
                for t in range(TILES):
                    dst = post_ps[:, t * EXPERTS:(t + 1) * EXPERTS]
                    nc.tensor.matmul(dst, before[:], chosen[:, t], start=True, stop=False)
                    if t == 1:
                        nc.tensor.matmul(dst, ones[:], chosen[:, 0], start=False, stop=False)
                    last = nc.tensor.matmul(dst, ones[:], counts[:], start=False, stop=True)
                last.then_inc(loc_mm, 1)

            def turn_kept(batch):
                wait(pe, keptb_ready, batch)
                for t in range(TILES):
                    last = nc.tensor.transpose(y_ps[:, :].bitcast(BF16)[0:BIAS_ROWS, t * P:(t + 1) * P],
                                               kept_b[:, t].rearrange("z i c -> z (i c)"), identb[:])
                last.then_inc(keptT_mm, 1)

            def expert_bias(batch):
                wait(pe, keptT_ready, batch)
                for t in range(TILES):
                    last = nc.tensor.matmul(y_ps[:, t * D:(t + 1) * D], keptT[:, t * P:(t + 1) * P], be_stack[:],
                                            start=True, stop=True)
                last.then_inc(bias_mm, 1)

            def expert(batch, par, r):
                t, first = r // 2, 4 * (r % 2)
                if at(batch, NB - 1):
                    wait(pe, x2T_ready, batch)
                    wait(pe, scaled_ready, batch - 1, (r + 2) % 4 + 1, 4)
                elif at(batch, NB - 2):
                    wait(pe, peak_read, NB - 1, UNITS, UNITS)
                    wait(pe, exp_ready, NB - 1, UNITS, UNITS)
                elif r == 0:
                    wait(pe, base_ready, batch)
                else:
                    wait(pe, scaled_ready, batch, r, 4)
                nc.tensor.matmul(y_bank(batch, r)[:], x2T[par][:, t * P:(t + 1) * P],
                                 weT[:, first:first + 4].rearrange("z e d -> z (e d)"), start=True, stop=True).then_inc(y_mm, 1)

            def step(n, cur, two):
                nxt = 1 - cur
                if at(n, 1):
                    pe.wait_ge(be_ready, 3)
                if at(n, 0):
                    pe.wait_ge(weT_ready, 2)
                front, par, pair = front_of(n, cur, two)
                if at(n, -1):
                    turn_front(1, 1, 0)
                    project_qk(1, 1)
                    project_v(0, 0)
                    turn_front(2, 0, 1)
                    project_qk(2, 0)
                for s in range(UNITS):
                    if live(n + 1):
                        peak(n + 1, nxt, s)
                    if live(n):
                        scores(n, cur, s)
                    if s == 0 and live(n - 2) and not at(n, NB + 1):
                        locate(n - 2)
                    if s == 3 and live(n):
                        turn_max(n, 1)
                    if s == 1 and live(n - 1):
                        values(n - 1, nxt, 3)
                    if s in VALUES_AT and live(n):
                        values(n, cur, VALUES_AT.index(s))
                    if s == 3 and live(n - 2) and not at(n, NB + 1):
                        turn_kept(n - 2)
                    if s == 3 and live(n - 1):
                        turn_o(n - 1)
                    if s == 4 and front is not None:
                        turn_front(front, par, pair)
                    if s == 5 and live(n - 2) and not at(n, NB + 1):
                        expert_bias(n - 2)
                    if s == 6 and live(n - 1):
                        turn_attn(n - 1)
                    if s == 6 and front is not None:
                        project_qk(front, par)
                    if s == 8 and live(n - 1):
                        project_o(n - 1)
                    if s == 9 and live(n + 1):
                        if at(n, -1):
                            pe.wait_ge(const_ready, 10)
                            pe.wait_ge(small_in, 5 * DMA)
                        turn_max(n + 1, 0)
                    if s in EXPERT_AT and live(n - 2) and not at(n, NB + 1):
                        expert(n - 2, cur, EXPERT_AT.index(s))
                    if s == 11 and live(n - 1):
                        turn_x2(n - 1)
                    if s == 12 and live(n + 1) and not at(n, -1):
                        project_v(n + 1, nxt)
                    if s == 13 and live(n - 1):
                        route(n - 1, nxt)
                if at(n, NB):
                    for r in (2, 3, 0, 1):
                        expert(n - 1, nxt, r)
                        if r == 2:
                            locate(n - 1)
                        elif r == 3:
                            turn_kept(n - 1)
                        elif r == 0:
                            expert_bias(n - 1)
                if at(n, -2):
                    late_setup()

            steps(pe, step)


_INS = ['x', 'ctx_1024', 'g_xattn', 'g_ffn', 'L0_xattn_Wq', 'L0_xattn_bq', 'L0_xattn_Wk', 'L0_xattn_bk',
        'L0_xattn_Wv', 'L0_xattn_bv', 'L0_xattn_Wo', 'L0_xattn_bo', 'L0_ffn_wg', 'L0_ffn_W', 'L0_ffn_b']


def kernel(**inputs):
    import numpy as _np
    import concourse.bacc as _bacc
    from concourse.bass_utils import run_bass_kernel_spmd as _run

    nc = _bacc.Bacc("TRN2", target_bir_lowering=False, num_devices=1)
    arrays, args = {}, []
    for name in _INS:
        a = _np.ascontiguousarray(inputs[name])
        arrays[f"in_{name}"] = a
        args.append(nc.dram_tensor(f"in_{name}", a.shape, mybir.dt.from_np(a.dtype), kind="ExternalInput").ap())
    o = nc.dram_tensor("out_0", (NB, SEQ, D), F32, kind="ExternalOutput").ap()
    build(nc, *args, o)
    r = _run(nc, [arrays], core_ids=[0])
    return r.results[0]["out_0"]
```
